# Optimizing a Trainium2 kernel written in Bass

```python
import numpy as np
import jax
import jax.numpy as jnp

def _softmax(x, axis=-1):
    return jax.nn.softmax(x, axis=axis)

def _gelu(x):
    return jax.nn.gelu(x, approximate=True)

def _silu(x):
    return jax.nn.silu(x)

def _sigmoid(x):
    return jax.nn.sigmoid(x)

def _layernorm(x, axis=-1, eps=1e-05):
    m = jnp.mean(x, axis=axis, keepdims=True)
    v = jnp.var(x, axis=axis, keepdims=True)
    return (x - m) / jnp.sqrt(v + eps)

def _scatter_add(tgt, idx, src, axis=0):
    return tgt.at[idx].add(src)

def _segment_sum(src, seg, n):
    return jax.ops.segment_sum(src, seg, n)
kernel_name = 'mk_decoder_postln_d1_seqx_r8_27a9ef'

def setup_inputs(seed: int=0):
    np.random.seed(seed)
    _w = jnp.asarray

    def _rec_inputs():
        import jax
        import jax.numpy as jnp
        _rk = jax.random.key(seed)
        x = 7.22e-05 + 1 * jax.random.normal(jax.random.fold_in(_rk, 1), (32, 128, 128), jnp.float32)
        _lenS = 128 - jax.random.randint(jax.random.fold_in(_rk, 7), (32,), 0, max(1, 128 // 4) + 1, jnp.int32)
        _lenS2 = 128 - jax.random.randint(jax.random.fold_in(_rk, 8), (32,), 0, max(1, 128 // 4) + 1, jnp.int32)
        _ctx_1024P = jax.random.normal(jax.random.fold_in(_rk, 11), (32, 16, 128), jnp.float32)
        _ctx_1024c = jax.random.dirichlet(jax.random.fold_in(_rk, 511), 0.3 * jnp.ones((16,), jnp.float32), (32, 128))
        _ctx_1024t = jnp.einsum('bsk,bkd->bsd', _ctx_1024c, _ctx_1024P)
        _ctx_1024t = _ctx_1024t * jax.lax.rsqrt(jnp.mean(jnp.square(_ctx_1024t)) + 1e-12) * 0.953939
        ctx_1024 = 4.13588e-05 + 0.999923 * (_ctx_1024t + 0.3 * jax.random.normal(jax.random.fold_in(_rk, 611), (32, 128, 128), jnp.float32))
        return (x, ctx_1024)
    x, ctx_1024 = _rec_inputs()

    def _L0_attn_setup():
        import jax, jax.numpy as jnp
        import numpy as np
        D_CONV = 4

        def _mamba_fwd(x, W_in, conv_w, conv_b, W_x, W_dt, b_dt, A_log, D_skip, W_out):
            Bsz, L, _ = x.shape
            d_inner, d_state = A_log.shape
            dt_rank = W_dt.shape[1]
            xz = x @ W_in.T
            xc, z = jnp.split(xz, 2, axis=-1)
            xt = xc.transpose(0, 2, 1)
            xt = jax.lax.conv_general_dilated(xt, conv_w, window_strides=(1,), padding=[(D_CONV - 1, 0)], feature_group_count=d_inner, dimension_numbers=('NCH', 'OIH', 'NCH'))
            xc = xt.transpose(0, 2, 1) + conv_b
            xc = jax.nn.silu(xc)
            xc = xc * 0 + 1
            dBC = xc @ W_x.T
            dlt = dBC[..., :dt_rank]
            Bm = dBC[..., dt_rank:dt_rank + d_state]
            Cm = dBC[..., dt_rank + d_state:]
            delta = jax.nn.softplus(dlt @ W_dt.T + b_dt)
            A = -jnp.exp(A_log)

            def step(h, inp):
                x_t, d_t, B_t, C_t = inp
                dA = jnp.exp(d_t[:, :, None] * A)
                dBx = d_t[:, :, None] * B_t[:, None, :] * x_t[:, :, None]
                h = dA * h + dBx
                y_t = jnp.einsum('ben,bn->be', h, C_t)
                return (h, y_t)
            h0 = jnp.zeros((Bsz, d_inner, d_state), x.dtype)
            xs = (xc.transpose(1, 0, 2), delta.transpose(1, 0, 2), Bm.transpose(1, 0, 2), Cm.transpose(1, 0, 2))
            _, ys = jax.lax.scan(step, h0, xs)
            y = ys.transpose(1, 0, 2) + D_skip * xc
            out = y * jax.nn.silu(z) @ W_out.T
            return out
        key = jax.random.key(seed)
        ks = jax.random.split(key, 10)
        d_model, d_inner, d_state, dt_rank = (128, 256, 16, 64)
        B, L = (2, 256)
        s = 0.02
        return {'x': jax.random.normal(ks[0], (B, L, d_model), jnp.float32), 'W_in': jax.random.normal(ks[1], (2 * d_inner, d_model), jnp.float32) * s, 'conv_w': jax.random.normal(ks[2], (d_inner, 1, D_CONV), jnp.float32) * s, 'conv_b': jax.random.normal(ks[3], (d_inner,), jnp.float32) * s, 'W_x': jax.random.normal(ks[4], (dt_rank + 2 * d_state, d_inner), jnp.float32) * s, 'W_dt': jax.random.normal(ks[5], (d_inner, dt_rank), jnp.float32) * s, 'b_dt': jax.random.normal(ks[6], (d_inner,), jnp.float32) * s, 'A_log': jnp.log(jnp.tile(jnp.arange(1, d_state + 1, dtype=jnp.float32), (d_inner, 1))), 'D_skip': jax.random.normal(ks[7], (d_inner,), jnp.float32), 'W_out': jax.random.normal(ks[8], (d_model, d_inner), jnp.float32) * s}
    _L0_attn_all = _L0_attn_setup()
    _L0_attn_in = {k: v for k, v in _L0_attn_all.items() if k in ('W_in', 'conv_w', 'conv_b', 'W_x', 'W_dt', 'b_dt', 'A_log', 'D_skip', 'W_out')}
    del _L0_attn_all

    def _L0_xattn_setup():
        import jax, jax.numpy as jnp
        import numpy as np
        DIM = 128
        HEAD_NUM = 8
        D_HEAD = DIM // HEAD_NUM
        B, S = (4, 256)
        key = jax.random.key(seed)
        ks = jax.random.split(key, 7)
        scale = 0.02
        return {'Q': jax.random.normal(ks[0], (B, S, DIM), dtype=jnp.float32), 'K': jax.random.normal(ks[1], (B, S, DIM), dtype=jnp.float32), 'V': jax.random.normal(ks[2], (B, S, DIM), dtype=jnp.float32), 'W_Q': jax.random.normal(ks[3], (DIM, DIM), dtype=jnp.float32) * scale, 'W_K': jax.random.normal(ks[4], (DIM, DIM), dtype=jnp.float32) * scale, 'W_V': jax.random.normal(ks[5], (DIM, DIM), dtype=jnp.float32) * scale, 'W_O': jax.random.normal(ks[6], (DIM, DIM), dtype=jnp.float32) * scale}
    _L0_xattn_all = _L0_xattn_setup()
    _L0_xattn_in = {k: v for k, v in _L0_xattn_all.items() if k in ('W_Q', 'W_K', 'W_V', 'W_O')}
    del _L0_xattn_all

    def _L0_ffn_setup():
        import jax, jax.numpy as jnp
        import numpy as np
        E, D, F, GATE_DIM = (8, 128, 512, 16)
        B, T = (2, 256)
        key = jax.random.key(seed)
        ks = jax.random.split(key, 7)
        s = 0.02
        return {'hidden_states': jax.random.normal(ks[0], (B, T, D), dtype=jnp.float32), 'w_red': jax.random.normal(ks[1], (D, GATE_DIM), dtype=jnp.float32) * s, 'wg': jax.random.normal(ks[2], (E, GATE_DIM), dtype=jnp.float32), 'w1': jax.random.normal(ks[3], (E, D, F), dtype=jnp.float32) * s, 'b1': jax.random.normal(ks[4], (E, F), dtype=jnp.float32) * s, 'w2': jax.random.normal(ks[5], (E, F, D), dtype=jnp.float32) * s, 'b2': jax.random.normal(ks[6], (E, D), dtype=jnp.float32) * s}
    _L0_ffn_all = _L0_ffn_setup()
    _L0_ffn_in = {k: v for k, v in _L0_ffn_all.items() if k in ('w_red', 'wg', 'w1', 'b1', 'w2', 'b2')}
    del _L0_ffn_all
    return {'x': x, 'ctx_1024': ctx_1024, 'L0_attn_W_in': _L0_attn_in['W_in'], 'L0_attn_conv_w': _L0_attn_in['conv_w'], 'L0_attn_conv_b': _L0_attn_in['conv_b'], 'L0_attn_W_x': _L0_attn_in['W_x'], 'L0_attn_W_dt': _L0_attn_in['W_dt'], 'L0_attn_b_dt': _L0_attn_in['b_dt'], 'L0_attn_A_log': _L0_attn_in['A_log'], 'L0_attn_D_skip': _L0_attn_in['D_skip'], 'L0_attn_W_out': _L0_attn_in['W_out'], 'L0_xattn_W_Q': _L0_xattn_in['W_Q'], 'L0_xattn_W_K': _L0_xattn_in['W_K'], 'L0_xattn_W_V': _L0_xattn_in['W_V'], 'L0_xattn_W_O': _L0_xattn_in['W_O'], 'L0_ffn_w_red': _L0_ffn_in['w_red'], 'L0_ffn_wg': _L0_ffn_in['wg'], 'L0_ffn_w1': _L0_ffn_in['w1'], 'L0_ffn_b1': _L0_ffn_in['b1'], 'L0_ffn_w2': _L0_ffn_in['w2'], 'L0_ffn_b2': _L0_ffn_in['b2']}

def reference(x, ctx_1024, L0_attn_W_in, L0_attn_conv_w, L0_attn_conv_b, L0_attn_W_x, L0_attn_W_dt, L0_attn_b_dt, L0_attn_A_log, L0_attn_D_skip, L0_attn_W_out, L0_xattn_W_Q, L0_xattn_W_K, L0_xattn_W_V, L0_xattn_W_O, L0_ffn_w_red, L0_ffn_wg, L0_ffn_w1, L0_ffn_b1, L0_ffn_w2, L0_ffn_b2):
    import jax
    import jax.numpy as jnp

    def _L0_attn_ref(x, W_in, conv_w, conv_b, W_x, W_dt, b_dt, A_log, D_skip, W_out):
        import jax, jax.numpy as jnp
        import numpy as np
        D_CONV = 4

        def _mamba_fwd(x, W_in, conv_w, conv_b, W_x, W_dt, b_dt, A_log, D_skip, W_out):
            Bsz, L, _ = x.shape
            d_inner, d_state = A_log.shape
            dt_rank = W_dt.shape[1]
            xz = x @ W_in.T
            xc, z = jnp.split(xz, 2, axis=-1)
            xt = xc.transpose(0, 2, 1)
            xt = jax.lax.conv_general_dilated(xt, conv_w, window_strides=(1,), padding=[(D_CONV - 1, 0)], feature_group_count=d_inner, dimension_numbers=('NCH', 'OIH', 'NCH'))
            xc = xt.transpose(0, 2, 1) + conv_b
            xc = jax.nn.silu(xc)
            xc = xc * 0 + 1
            dBC = xc @ W_x.T
            dlt = dBC[..., :dt_rank]
            Bm = dBC[..., dt_rank:dt_rank + d_state]
            Cm = dBC[..., dt_rank + d_state:]
            delta = jax.nn.softplus(dlt @ W_dt.T + b_dt)
            A = -jnp.exp(A_log)

            def step(h, inp):
                x_t, d_t, B_t, C_t = inp
                dA = jnp.exp(d_t[:, :, None] * A)
                dBx = d_t[:, :, None] * B_t[:, None, :] * x_t[:, :, None]
                h = dA * h + dBx
                y_t = jnp.einsum('ben,bn->be', h, C_t)
                return (h, y_t)
            h0 = jnp.zeros((Bsz, d_inner, d_state), x.dtype)
            xs = (xc.transpose(1, 0, 2), delta.transpose(1, 0, 2), Bm.transpose(1, 0, 2), Cm.transpose(1, 0, 2))
            _, ys = jax.lax.scan(step, h0, xs)
            y = ys.transpose(1, 0, 2) + D_skip * xc
            out = y * jax.nn.silu(z) @ W_out.T
            return out
        return _mamba_fwd(x, W_in, conv_w, conv_b, W_x, W_dt, b_dt, A_log, D_skip, W_out)

    def _L0_xattn_ref(Q, K, V, W_Q, W_K, W_V, W_O):
        import jax, jax.numpy as jnp
        import numpy as np
        DIM = 128
        HEAD_NUM = 8
        D_HEAD = DIM // HEAD_NUM
        B, S = (4, 256)
        b, s, d = Q.shape
        h, dh = (HEAD_NUM, d // HEAD_NUM)

        def proj_split(x, W):
            y = jnp.einsum('bsd,ed->bse', x, W)
            return y.reshape(b, s, h, dh).transpose(0, 2, 1, 3)
        q = proj_split(Q, W_Q)
        k = proj_split(K, W_K)
        v = proj_split(V, W_V)
        scores = jnp.einsum('bhqd,bhkd->bhqk', q, k) / jnp.sqrt(jnp.float32(dh))
        attn = jax.nn.softmax(scores, axis=1)
        ctx = jnp.einsum('bhqk,bhkd->bhqd', attn, v)
        ctx = ctx.transpose(0, 2, 1, 3).reshape(b, s, d)
        return jnp.einsum('bsd,ed->bse', ctx, W_O)

    def _L0_ffn_ref(hidden_states, w_red, wg, w1, b1, w2, b2):
        import jax, jax.numpy as jnp
        import numpy as np
        E, D, F, GATE_DIM = (8, 128, 512, 16)
        B, T = (2, 256)
        b, t, c = hidden_states.shape
        x = hidden_states.reshape(-1, c)
        red = x @ w_red
        wg_n = wg / jnp.maximum(jnp.linalg.norm(wg, axis=1, keepdims=True), 0.0001)
        logits = red @ wg_n.T
        gates = jax.nn.softmax(logits, axis=1)
        idx = jnp.argmax(gates, axis=1)
        scores = jnp.take_along_axis(gates, idx[:, None], axis=1)
        h = jax.nn.gelu(jnp.einsum('td,edf->etf', x, w1) + b1[:, None, :], approximate=False)
        y = jnp.einsum('etf,efd->etd', h, w2) + b2[:, None, :]
        out = jnp.take_along_axis(y, idx[None, :, None], axis=0)[0]
        out = out * scores
        return out.reshape(b, t, c)
    x = _layernorm(x + _L0_attn_ref(x, L0_attn_W_in, L0_attn_conv_w, L0_attn_conv_b, L0_attn_W_x, L0_attn_W_dt, L0_attn_b_dt, L0_attn_A_log, L0_attn_D_skip, L0_attn_W_out), axis=-1)
    x = _layernorm(x + _L0_xattn_ref(x, ctx_1024, ctx_1024, L0_xattn_W_Q, L0_xattn_W_K, L0_xattn_W_V, L0_xattn_W_O), axis=-1)
    x = _layernorm(x + _L0_ffn_ref(x, L0_ffn_w_red, L0_ffn_wg, L0_ffn_w1, L0_ffn_b1, L0_ffn_w2, L0_ffn_b2), axis=-1)
    return x

_drawn_inputs = setup_inputs


def setup_inputs(seed=0):
    import zlib

    import numpy as np

    out = dict(_drawn_inputs(seed))
    spreads = {}
    factors = {'L0_attn_W_x': 8.0,
     'L0_attn_W_dt': 8.0,
     'L0_attn_b_dt': 8.0,
     'L0_attn_A_log': 8.0,
     'L0_xattn_W_Q': 4.618,
     'L0_xattn_W_K': 4.65,
     'L0_ffn_w_red': 6.311,
     'L0_ffn_wg': 6.303,
     'L0_ffn_w1': 6.41,
     'L0_ffn_b1': 8.0,
     'L0_ffn_w2': 6.278,
     'L0_ffn_b2': 8.0}
    for name, (base, spread) in spreads.items():
        noise = np.random.default_rng([zlib.crc32(name.encode()), seed]).standard_normal(out[name].shape)
        drawn = base * np.exp(spread * noise) if base else spread * noise
        out[name] = jnp.asarray(drawn.astype(out[name].dtype))
    for name, factor in factors.items():
        out[name] = (out[name] * factor).astype(out[name].dtype)
    return out
```

```python
from contextlib import ExitStack

import numpy as np

import concourse.bass as bass
from concourse import mybir

ALU = mybir.AluOpType
ACT = mybir.ActivationFunctionType
AX = mybir.AxisListType
F32 = mybir.dt.float32
BF16 = mybir.dt.bfloat16
I32 = mybir.dt.int32
U32 = mybir.dt.uint32

P = 128
NSEQ = 32
UB = 4
UN = NSEQ // UB
UT = UB * P
H, DH = 8, 16
EI, NST, RANK = 256, 16, 64
NE, FF = 8, 512
FC = FF // P
TOK = NSEQ * P
CAP = TOK + P
ROW = P + 2
NT = TOK // P + NE - 1
GT = 3
NG = NT // GT
QR = P // UB
EPS = 1e-5


def at_least(eng, sem, n):
    if isinstance(n, int) and n <= 0:
        return
    eng.wait_ge(sem, n)


def wait_apart(eng, sem, n, met):
    if isinstance(n, int):
        return at_least(eng, sem, n)
    n = eng.snap(n)
    eng.wait_ge(met, 1)
    eng.wait_ge(sem, n)


class Chain:

    def __init__(self, eng, sem):
        self.eng, self.sem, self.done, self.n = eng, sem, 0, 0

    def __call__(self, ins, met=None):
        self.n += 1
        ins.then_inc(self.sem, 1)
        if met:
            wait_apart(self.eng, self.sem, self.done + self.n, met)
        else:
            self.eng.wait_ge(self.sem, self.done + self.n)

    def enter(self, rounds, per_round):
        self.before, self.per_round = self.done + self.n, per_round
        self.done, self.n = self.before + rounds * per_round, 0

    def leave(self, rounds):
        assert self.n == self.per_round, f"a round has {self.n} steps"
        self.done, self.n = self.before + rounds * self.per_round, 0


def decoder_program(nc, x_t, x_tok, ctx_t, wz_t, wx_t, wdt_t, small, a_log, wout_t, wqkvo_t,
                    wred_t, wg, w1, w2, b12, consts, out):
    ctx = ExitStack()
    with ctx:
        def sb(name, shape, dt=F32):
            return ctx.enter_context(nc.sbuf_tensor(name, shape, dt))

        def sem(name):
            return ctx.enter_context(nc.semaphore(name))

        lists = nc.dram_tensor("expert_lists", [(NE + 1) * CAP, ROW], F32, kind="Internal").ap()
        bias_parts = nc.dram_tensor("bias_parts", [3, NE * (FF + P)], BF16, kind="Internal").ap()

        ps = ctx.enter_context(nc.psum_tensor("ps", [P, 8, 512], F32))
        W0, W1, W2, CT = ps[:, 4, :], ps[:, 5, :], ps[:, 6, :], ps[:, 7, :]

        wz = sb("wz", [P, EI]); wx = sb("wx", [P, 2, 96]); wdt = sb("wdt", [RANK, EI])
        sm = sb("sm", [P, 4])
        alog = sb("alog", [P, 2, NST]); wout = sb("wout", [P, 2, P])
        wqkvo = sb("wqkvo", [P, 4, P]); wred = sb("wred", [16, P]); wgs = sb("wgs", [NE, 16])
        w1s = sb("w1s", [P, NE * FF]); w2s = sb("w2s", [P, NE * FC * P])
        CW = 128 * 3 + 8 + 32 + 4 + 39 * 8 + 4
        cst = sb("cst", [P, CW])
        o = 0
        ident = cst[:, o:o + P]; o += P
        negi = cst[:, o:o + P]; o += P
        before_f = cst[:, o:o + P]; o += P
        hmask = cst[:, o:o + H]; o += H
        rank = cst[:, o:o + UB * NE]; o += UB * NE
        ids = cst[:, o:o + UB]; o += UB
        tnum = cst[0:1, o:o + NT * NE]; o += NT * NE
        ones_c = cst[:, o:o + 1]; mhalf = cst[:, o + 1:o + 2]; o += 4

        ones_b = sb("ones_b", [P, P], BF16); before = sb("before", [P, P], BF16)
        ones3 = sb("ones3", [P, P], BF16)
        ones_f = sb("ones_f", [P, P])
        mh = sb("mh", [P, 4])

        dbc = sb("dbc", [P, 96]); dlt = sb("dlt", [RANK, 1])
        v = sb("v", [P, 14, 2]); dn = sb("dn", [P, 8, 2 * NST])
        yd = sb("yd", [P, 2, P]); wsum = sb("wsum", [P, 2, P])
        wr = sb("wr", [P, NE]); g8 = sb("g8", [NE, 20]); wgT = sb("wgT", [16, NE])
        xt = sb("xt", [P, 2, UT]); xk = sb("xk", [P, 2, UT]); ct_in = sb("ct_in", [P, 2, UT])
        th = sb("th", [P, 2, UT]); g = sb("g", [P, 2, UT])
        xs = sb("xs", [P, UB, P]); st = sb("st", [P, UB, 6]); mv = sb("mv", [P, 5, UB])
        ve = sb("ve", [P, UB]); rs = sb("rs", [P, UB]); nb = sb("nb", [P, UB])
        xs2 = sb("xs2", [P, UB, P]); st2 = sb("st2", [P, UB, 6]); mv2 = sb("mv2", [P, 5, UB])
        ve2 = sb("ve2", [P, UB]); rs2 = sb("rs2", [P, UB]); nb2 = sb("nb2", [P, UB])
        x1 = sb("x1", [P, UB, P]); x1r = sb("x1r", [P, 2, UB, P]); x1T = sb("x1T", [P, UT])
        qbd = sb("qbd", [P, 2, H, UB, P]); kt = sb("kt", [P, UB, P])
        VW = H * (P + DH)
        vbd = sb("vbd", [P, 2, UB, VW])
        mx = sb("mx", [P, 2, P]); E = sb("E", [P, 4, H, P]); se = sb("se", [P, 2, P])
        pw = E[:, :, :, :].rearrange("p j h q -> p (j h) q")
        re = sb("re", [P, 2, P]); ctT = sb("ctT", [P, UB, P])
        x2 = sb("x2", [P, 2, UB, ROW]); x2T = sb("x2T", [P, UB, P])
        df = sb("df", [P, UB, NE]); er = sb("er", [P, UB, NE]); rk = sb("rk", [P, UB, NE])
        r4 = sb("r4", [P, 6, UB]); oh = sb("oh", [P, UB, NE], BF16)
        seen = sb("seen", [P, 2, NE], BF16); cu = sb("cu", [P, NE]); pr = sb("pr", [P, UB, NE])
        idx = sb("idx", [P, 2, UB], U32)
        pad = sb("pad", [P, ROW]); tailx = sb("tailx", [QR, UB], U32)
        tb = sb("tb", [1, 12, NT]); cn = sb("cn", [P, 8, NE]); cni = sb("cni", [1, NE], I32)
        ge = sb("ge", [1, 2, NT * NE]); tab = sb("tab", [1, 2, NT], I32); pidx = sb("pidx", [P, NE], U32)
        BW = NE * (FF + P) // P
        bf = sb("bf", [P, 3, BW]); bp = sb("bp", [P, 3, BW], BF16)
        bias = sb("bias", [P, NE * (FF + P)], BF16)
        NX = 2 * GT
        xr = sb("xr", [P, NX, ROW]); xrT = sb("xrT", [P, GT, P])
        q0 = qbd[:, 0, :, :, :].rearrange("p h b q -> p (h b q)")
        q1 = qbd[:, 1, :, :, :].rearrange("p h b q -> p (h b q)")
        hg = q0[:, 0:GT * FF].rearrange("p (s f) -> p s f", s=GT)
        hT = q0[:, GT * FF:2 * GT * FF].rearrange("p (s f) -> p s f", s=GT)
        rsd = q1[:, 0:NX * P].rearrange("p (s f) -> p s f", s=NX)
        ot = q1[:, NX * P:2 * NX * P].rearrange("p (s f) -> p s f", s=NX)
        tix = sb("tix", [P, NX], U32)
        st3 = sb("st3", [P, NX, 6]); mv3 = sb("mv3", [P, 5, NX])
        ve3 = sb("ve3", [P, NX]); rs3 = sb("rs3", [P, NX]); nb3 = sb("nb3", [P, NX])

        S = {n: sem(n) for n in (
            "consts_in weights_in experts_in bias_in bias_out bias_back memset_done ones_done mix_rows mix_rows_copied "
            "delta_pre delta_raw exp_a exp_b ln_c dax yd_ready router_norm router_pow wg_turned wgT_ready "
            "router_mm wr_ready "
            "z_ready tanh_ready u_ready g_ready mixed ln1_var ln1_rstd ln1_shift x1_ready x1_kept x1T_ready "
            "x1T_copied q_ready qbd_ready k_ready k_copied v_ready v_copied "
            "scores max_ready shifted exp_ready recip_ready attn_ready ctx_ready ctx_copied "
            "proj ln2_sum ln2_var ln2_rstd ln2_shift x2_ready x2T_ready x2T_copied logits diff_ready "
            "gate_exp onehot pos_ready idx_ready pads_out pad_ready counts table_ready "
            "dve act pool rowT rowT_copied hidden gelu hidT hidT_copied y_ready res_ready var3 rstd3 "
            "shift3 out_ready tix_ready").split()}
        xt_in = [sem(f"xt_in{p}") for p in range(2)]
        xk_in = [sem(f"xk_in{p}") for p in range(2)]
        ct_in_s = [sem(f"ctx_in{p}") for p in range(2)]
        rows_out = [sem(f"rows_out{k}") for k in range(2 * UB)]
        rows_in = [sem(f"rows_in{k}") for k in range(NX)]
        final_out = [sem(f"final_out{k}") for k in range(NX)]

        def schedule(eng, unit, chain=None, per_round=0):
            for a in (-2, -1, 0, 1):
                unit(a, a // 2, a % 2, range(a, a + 1))
            with eng.Fori(1, 3) as k:
                if chain:
                    chain.enter(k - 1, per_round)
                unit(2 * k, k, 0, range(2, 5))
                unit(2 * k + 1, k, 1, range(3, 6))
                if chain:
                    chain.leave(2)
            for a in (6, 7, 8, 9):
                unit(a, a // 2, a % 2, range(a, a + 1))

        def runs(which, shift):
            return 0 <= which[0] + shift < UN

        def schedule2(eng, group, chain=None, per_round=0):
            for n in range(5):
                group(n, n // 2, n % 2)
            with eng.Fori(2, NG // 2 - 1) as k:
                if chain:
                    chain.enter(k - 2, per_round)
                group(2 * k + 1, k, 1)
                group(2 * k + 2, k + 1, 0)
                if chain:
                    chain.leave(NG // 2 - 3)
            for n in range(NG - 2, NG + 2):
                group(n, n // 2, n % 2)

        block = ctx.enter_context(nc.Block())

        @block.sync
        def _(sp):
            def load(n, par):
                cols = bass.ds(n * UT, UT)
                at_least(sp, S["z_ready"], n - 1 if not isinstance(n, int) or n > 1 else 0)
                sp.dma_start(xt[:, par, :], x_t[:, cols]).then_inc(xt_in[par], 16)
                at_least(sp, S["ln1_var"], n - 1 if not isinstance(n, int) or n > 1 else 0)
                sp.dma_start(xk[:, par, :], x_tok[:, cols]).then_inc(xk_in[par], 16)
                at_least(sp, S["v_ready"], n - 1 if not isinstance(n, int) or n > 1 else 0)
                sp.dma_start(ct_in[:, par, :], ctx_t[:, cols]).then_inc(ct_in_s[par], 16)

            sp.dma_start(wx[:, :, :], wx_t).then_inc(S["consts_in"], 16)
            sp.dma_start(wdt[:, :], wdt_t).then_inc(S["consts_in"], 16)
            sp.dma_start(sm[:, :], small).then_inc(S["consts_in"], 16)
            sp.dma_start(alog[:, :, :], a_log).then_inc(S["consts_in"], 16)
            sp.dma_start(cst[:, :], consts).then_inc(S["consts_in"], 16)
            sp.dma_start(wz[:, :], wz_t).then_inc(S["weights_in"], 16)
            load(0, 0)
            sp.dma_start(wout[:, :, :], wout_t).then_inc(S["weights_in"], 16)
            sp.dma_start(wqkvo[:, :, :], wqkvo_t).then_inc(S["weights_in"], 16)
            sp.dma_start(wred[:, :], wred_t).then_inc(S["weights_in"], 16)
            sp.dma_start(wgs[:, :], wg).then_inc(S["weights_in"], 16)
            load(1, 1)
            sp.dma_start(bf[:, 0, :], b12).then_inc(S["bias_in"], 16)
            sp.dma_start(w1s[:, :], w1).then_inc(S["experts_in"], 16)
            sp.dma_start(w2s[:, :], w2).then_inc(S["experts_in"], 16)
            sp.wait_ge(S["bias_out"], 1)
            sp.dma_start(bias_parts.rearrange("k (p f) -> p k f", p=P), bp[:, :, :]).then_inc(S["bias_back"], 16)
            sp.wait_ge(S["bias_back"], 16)
            sp.dma_start(bias[0:3, :], bias_parts).then_inc(S["bias_back"], 16)
            with sp.Fori(1, UN // 2) as k:
                load(2 * k, 0)
                load(2 * k + 1, 1)

            sp.wait_ge(S["table_ready"], 1)
            for n, q in enumerate(rows_out):
                sp.wait_ge(q, 16 * (UN // 2 + n // UB))
            sp.wait_ge(S["pads_out"], 16 * NE)

            def group(n, k, par):
                if isinstance(n, int) and n >= NG:
                    return
                for s in range(GT):
                    t = n * GT + s
                    slot = par * GT + s
                    if not (isinstance(n, int) and n < 2):
                        at_least(sp, S["res_ready"], t - NX + 1)
                    at = sp.value_load(tab[0:1, 0, bass.ds(t, 1)], min_val=0, max_val=NE * CAP)
                    sp.dma_start(xr[:, slot, :], lists[bass.ds(at, P), :]).then_inc(rows_in[slot], 16)

            group(0, 0, 0)
            group(1, 0, 1)
            with sp.Fori(1, (NG + 1) // 2 - 1) as k:
                group(2 * k, k, 0)
                group(2 * k + 1, k, 1)
            group(NG - 1, NG // 2, 0)

        @block.tensor
        def _(pe):
            mm, tr = nc.tensor.matmul, nc.tensor.transpose
            pe.wait_ge(S["consts_in"], 80)
            pe.wait_ge(S["ones_done"], 1)
            for c in range(2):
                mm(W0[:, 0:96], ones_f[:, :], wx[:, c, :], start=(c == 0), stop=(c == 1))
            for c in range(2):
                last = mm(W1[0:RANK, 0:1], wx[:, c, 0:RANK], ones_f[:, 0:1], start=(c == 0), stop=(c == 1))
            last.then_inc(S["mix_rows"], 1)
            pe.wait_ge(S["mix_rows_copied"], 1)
            for c in range(2):
                last = mm(W2[:, c:c + 1], wdt[:, c * P:(c + 1) * P], dlt[:, :], start=True, stop=True)
            last.then_inc(S["delta_raw"], 1)
            pe.wait_ge(S["router_norm"], 2)
            pe.wait_ge(S["weights_in"], 80)
            tr(CT[0:16, 0:NE], g8[:, 0:16], ident[0:NE, 0:NE]).then_inc(S["wg_turned"], 1)
            pe.wait_ge(S["wgT_ready"], 1)
            mm(CT[:, 16:16 + NE], wred[:, :], wgT[:, :], start=True, stop=True).then_inc(S["router_mm"], 1)

            def unit(a, k, par, which):
                m, q, r, z = a + 1, a - 1, a - 2, a + 2
                att, mix, post, route = (runs(which, x) for x in (0, 1, -1, -2))
                mp = 1 - par

                def score(i, first):
                    jj = first % UB
                    pp = par if first < UB else mp
                    if first == UB:
                        pe.wait_ge(S["qbd_ready"], m + 1)
                        pe.wait_ge(S["k_copied"], m + 1)
                    at_least(pe, S["exp_ready"], i - 1)
                    for hh in range(2):
                        last = mm(ps[:, 2 * (jj % 2) + hh, :], kt[:, jj, :],
                                  qbd[:, pp, 4 * hh:4 * hh + 4, jj, :], start=True, stop=False,
                                  skip_group_check=True)
                    last.then_inc(S["scores"], 1)

                for j in range(UB):
                    i = UB * a + j
                    if j == 0 and route:
                        pe.wait_ge(S["x2_ready"], r + 1)
                        pe.wait_ge(S["qbd_ready"], a + 1 if runs(which, 0) else UN)
                        at_least(pe, S["idx_ready"], r)
                        for t in range(UB):
                            last = tr(W2[:, t * P:(t + 1) * P], x2[:, par, t, 0:P], ident)
                        last.then_inc(S["x2T_ready"], 1)
                    if j < 3 and att:
                        score(i + 1, j + 1)
                    if j == 0 and mix:
                        pe.wait_ge(S["g_ready"], m + 1)
                        for b in range(UB):
                            for c in range(2):
                                last = mm(W0[:, b * P:(b + 1) * P], g[:, c, b * P:(b + 1) * P], wout[:, c, :],
                                          start=(c == 0), stop=(c == 1))
                        last.then_inc(S["mixed"], 1)
                    if att:
                        pe.wait_ge(S["max_ready"], i + 1)
                        for hh in range(2):
                            last = mm(ps[:, 2 * (j % 2) + hh, :], negi,
                                      mx[:, j % 2, :].unsqueeze(1).to_broadcast([P, 4, P]),
                                      start=False, stop=True, skip_group_check=True)
                        last.then_inc(S["shifted"], 1)
                    if (att and j >= 2) or (post and j < 2):
                        jj = (j - 2) % UB
                        vp = par if j >= 2 else mp
                        pe.wait_ge(S["attn_ready"], i - 1)
                        if j == 2:
                            pe.wait_ge(S["v_copied"], a + 1)
                            at_least(pe, S["ctx_copied"], a)
                        for h in range(H):
                            last = mm(CT[:, jj * P:(jj + 1) * P], vbd[:, vp, jj, h * P:(h + 1) * P],
                                      E[:, jj, h, :], start=(h == 0), stop=(h == H - 1))
                        last.then_inc(S["ctx_ready"], 1)
                    if j == 0 and route:
                        pe.wait_ge(S["x2T_copied"], r + 1)
                        for t in range(UB):
                            last = mm(W2[:, t * NE:(t + 1) * NE], x2T[:, t, :], wr[:, :], start=True, stop=True)
                        last.then_inc(S["logits"], 1)
                    if j == 1 and mix:
                        pass
                    if j == 1 and att:
                        pe.wait_ge(ct_in_s[par], (k + 1) * 16)
                        if mix:
                            pe.wait_ge(S["u_ready"], m + 1)
                        at_least(pe, S["ln2_sum"], a - 1)
                        for b in range(UB):
                            last = mm(W1[:, b * P:(b + 1) * P], ct_in[:, par, b * P:(b + 1) * P],
                                      wqkvo[:, 2, :], start=True, stop=True)
                        last.then_inc(S["v_ready"], 1)
                    if j == 1 and route:
                        pe.wait_ge(S["onehot"], r + 1)
                        kw = dict(skip_group_check=True)
                        pos = W2[:, UB * NE:2 * UB * NE]
                        mm(pos, before[:, :], oh[:, :, :], start=True, stop=False, **kw)
                        mm(pos, ones_b[:, :], seen[:, mp, :].unsqueeze(1).to_broadcast([P, UB, NE]),
                           start=False, stop=False, **kw)
                        for t in range(1, UB):
                            last = mm(pos[:, t * NE:], ones_b[:, :], oh[:, 0:UB - t, :],
                                      start=False, stop=(t == UB - 1), **kw)
                        last.then_inc(S["pos_ready"], 1)
                    if j == 1 and mix:
                        pe.wait_ge(S["x1_ready"], m + 1)
                        for b in range(UB):
                            last = tr(W0[:, b * P:(b + 1) * P], x1[:, b, :], ident)
                        last.then_inc(S["x1T_ready"], 1)
                    if j == 2 and post:
                        pe.wait_ge(S["ctx_copied"], q + 1)
                        if att:
                            pe.wait_ge(S["v_copied"], a + 1)
                        at_least(pe, S["ln2_sum"], q)
                        for b in range(UB):
                            last = mm(W1[:, b * P:(b + 1) * P], ctT[:, b, :], wqkvo[:, 3, :],
                                      start=True, stop=True)
                        last.then_inc(S["proj"], 1)
                    if j == 2 and mix:
                        if route:
                            pe.wait_ge(S["idx_ready"], r + 1)
                        pe.wait_ge(S["x1T_copied"], m + 1)
                        if which[0] == -1:
                            pe.wait_ge(S["router_mm"], 1)
                        mm(W2, wqkvo[:, 0, :], x1T[:, :], start=True, stop=True).then_inc(S["q_ready"], 1)
                        km = k if par == 0 else k + 1
                        pe.wait_ge(ct_in_s[mp], (km + 1) * 16)
                        mm(W0, wqkvo[:, 1, :], ct_in[:, mp, :], start=True, stop=True).then_inc(S["k_ready"], 1)
                    if j == 3 and runs(which, 2):
                        pe.wait_ge(xt_in[par], (k + 2) * 16)
                        if mix:
                            pe.wait_ge(S["k_copied"], m + 1)
                        if post:
                            pe.wait_ge(S["ln2_sum"], q + 1)
                        elif att:
                            pe.wait_ge(S["v_copied"], a + 1)
                        mm(W0, wz[:, 0:P], xt[:, par, :], start=True, stop=True)
                        mm(W1, wz[:, P:2 * P], xt[:, par, :], start=True, stop=True).then_inc(S["z_ready"], 1)
                    if j == 3 and mix:
                        score(i + 1, UB)

            schedule(pe, unit)

            pe.wait_ge(S["idx_ready"], UN)
            mm(W0[:, 0:NE], ones_b[:, :], seen[:, 1, :], start=True, stop=True).then_inc(S["counts"], 1)

            XT, Y = ps[:, 0, 0:P], ps[:, 7, 0:P]
            pe.wait_ge(S["table_ready"], 1)
            pe.wait_ge(S["experts_in"], 32)
            pe.wait_ge(S["bias_back"], 32)

            def turn_rows(t, k, slot):
                pe.wait_ge(rows_in[slot], 16 * (k + 1))
                at_least(pe, S["rowT_copied"], t)
                tr(XT, xr[:, slot, 0:P], ident).then_inc(S["rowT"], 1)

            turn_rows(0, 0, 0)

            def group(n, k, par):
                whole = isinstance(n, int)
                for s in range(GT):
                    t = n * GT + s
                    if not whole or t < NT:
                        e = pe.value_load(tab[0:1, 1, bass.ds(t, 1)], min_val=0, max_val=NE - 1)
                        if not whole or t >= GT:
                            at_least(pe, S["gelu"], t - GT + 1)
                        mm(ps[:, 1 + s, :], ones3[:, :], bias[:, bass.ds(e * FF, FF)], start=True, stop=False)
                        pe.wait_ge(S["rowT_copied"], t + 1)
                        mm(ps[:, 1 + s, :], xrT[:, s, :], w1s[:, bass.ds(e * FF, FF)],
                           start=False, stop=True).then_inc(S["hidden"], 1)
                    if not whole or (1 <= t < NT + 1):
                        sb_ = (s - 1) % GT
                        pe.wait_ge(S["gelu"], t)
                        if not whole or t - 1 >= GT:
                            at_least(pe, S["hidT_copied"], t - GT)
                        for c in range(FC):
                            last = tr(ps[:, 4 + sb_, c * P:(c + 1) * P], hg[:, sb_, c * P:(c + 1) * P], ident)
                        last.then_inc(S["hidT"], 1)
                    if not whole or (2 <= t < NT + 2):
                        sc = (s - 2) % GT
                        e = pe.value_load(tab[0:1, 1, bass.ds(t - 2, 1)], min_val=0, max_val=NE - 1)
                        if not whole or t > 2:
                            at_least(pe, S["res_ready"], t - 2)
                        mm(Y, ones3[:, :], bias[:, bass.ds(e * P + NE * FF, P)], start=True, stop=False)
                        pe.wait_ge(S["hidT_copied"], t - 1)
                        for c in range(FC):
                            last = mm(Y, hT[:, sc, c * P:(c + 1) * P], w2s[:, bass.ds(e * FF + c * P, P)],
                                      start=False, stop=(c == FC - 1))
                        last.then_inc(S["y_ready"], 1)
                    if not whole or t + 1 < NT:
                        if s < 2:
                            turn_rows(t + 1, k, par * GT + s + 1)
                        else:
                            turn_rows(t + 1, k if par == 0 else k + 1, (1 - par) * GT)

            schedule2(pe, group)

        @block.scalar
        def _(act):
            A = nc.scalar.activation
            link = Chain(act, S["act"])
            act.wait_ge(S["consts_in"], 80)
            link(A(dn[:, 0, :], alog[:, :, :].rearrange("p c n -> p (c n)"), ACT.Exp))
            act.wait_ge(S["delta_pre"], 1)
            A(v[:, 3, :], v[:, 2, :], ACT.Exp).then_inc(S["exp_a"], 1)
            act.wait_ge(S["exp_b"], 1)
            A(v[:, 5, :], v[:, 4, :], ACT.Ln).then_inc(S["ln_c"], 1)
            act.wait_ge(S["dax"], 1)
            A(dn[:, 3, :], dn[:, 2, :], ACT.Exp).then_inc(S["exp_a"], 1)

            def unit(a, k, par, which):
                m, q, r, z = a + 1, a - 1, a - 2, a + 2
                att, mix, post, route = (runs(which, x) for x in (0, 1, -1, -2))
                mp = 1 - par

                def exps(j):
                    i = UB * a + j
                    act.wait_ge(S["shifted"], i + 1)
                    at_least(act, S["ctx_ready"], i - 3)
                    pp = j % 2
                    A(E[:, j, :, :], ps[:, 2 * pp:2 * pp + 2, :], ACT.Exp).then_inc(S["exp_ready"], 1)

                def heads(h0, h1):
                    for h in range(h0, h1):
                        last = A(qbd[:, mp, h, :, :], W2, ACT.Identity, scale=hmask[:, h:h + 1])
                    return last

                if route:
                    act.wait_ge(S["x2T_ready"], r + 1)
                    at_least(act, S["logits"], r)
                    A(x2T[:, :, :], W2, ACT.Identity).then_inc(S["x2T_copied"], 1)
                if att:
                    exps(0)
                if att:
                    act.wait_ge(S["v_ready"], a + 1)
                    at_least(act, S["ctx_ready"], UB * (a - 1))
                    A(vbd[:, par, :, :].rearrange("p b (h w) -> p b h w", w=P + DH)[:, :, :, 0:DH],
                      W1, ACT.Identity).then_inc(S["v_copied"], 1)
                if mix:
                    act.wait_ge(S["ln1_shift"], m + 1)
                    at_least(act, S["x1T_ready"], m)
                    at_least(act, S["x1_kept"], m)
                    for b in range(UB):
                        last = A(x1[:, b, :], xs[:, b, :], ACT.Identity, bias=nb[:, b:b + 1], scale=rs[:, b:b + 1])
                    last.then_inc(S["x1_ready"], 1)
                if att:
                    exps(1)
                if post:
                    act.wait_ge(S["ctx_ready"], UB * a)
                    at_least(act, S["proj"], q)
                    A(ctT[:, :, :], CT, ACT.Identity).then_inc(S["ctx_copied"], 1)
                if route:
                    act.wait_ge(S["diff_ready"], r + 1)
                    A(er[:, :, :], df[:, :, :], ACT.Exp).then_inc(S["gate_exp"], 1)
                if mix:
                    act.wait_ge(S["x1T_ready"], m + 1)
                    at_least(act, S["q_ready"], m)
                    A(x1T[:, :], W0, ACT.Identity).then_inc(S["x1T_copied"], 1)
                if att:
                    exps(2)
                if mix:
                    act.wait_ge(S["q_ready"], m + 1)
                    at_least(act, S["scores"], UB * (m - 1) if not isinstance(m, int) or m > 1 else 0)
                    heads(0, 4)
                if mix:
                    act.wait_ge(S["k_ready"], m + 1)
                    at_least(act, S["scores"], UB * m)
                    A(kt[:, :, :], W0, ACT.Identity).then_inc(S["k_copied"], 1)
                if att:
                    exps(3)
                if mix:
                    heads(4, H).then_inc(S["qbd_ready"], 1)
                if post:
                    act.wait_ge(S["ln2_shift"], q + 1)
                    if not isinstance(q, int) or q >= 2:
                        for t in range(UB):
                            act.wait_ge(rows_out[mp * UB + t], 16 * k)
                    for b in range(UB):
                        last = A(x2[:, mp, b, 0:P], xs2[:, b, :], ACT.Identity, bias=nb2[:, b:b + 1],
                                 scale=rs2[:, b:b + 1])
                    last.then_inc(S["x2_ready"], 1)
                if runs(which, 2):
                    act.wait_ge(S["z_ready"], z + 1)
                    at_least(act, S["u_ready"], z)
                    A(th[:, :, :], ps[:, 4:6, :], ACT.Tanh, scale=0.5).then_inc(S["tanh_ready"], 1)

            schedule(act, unit)

            def group(n, k, par):
                whole = isinstance(n, int)
                if not whole or 2 <= n:
                    act.wait_ge(S["shift3"], n - 1)
                    for s in range(GT):
                        slot = par * GT + s
                        if not whole or n >= 4:
                            act.wait_ge(final_out[slot], 16 * (k - 1))
                        A(ot[:, slot, :], rsd[:, slot, :], ACT.Identity, bias=nb3[:, slot:slot + 1],
                          scale=rs3[:, slot:slot + 1]).then_inc(S["out_ready"], 1)
                for s in range(GT):
                    t = n * GT + s
                    if whole and t >= NT:
                        continue
                    act.wait_ge(S["rowT"], t + 1)
                    if not whole or t >= GT:
                        at_least(act, S["hidden"], t - GT + 1)
                    A(xrT[:, s, :], ps[:, 0, 0:P], ACT.Identity).then_inc(S["rowT_copied"], 1)
                    act.wait_ge(S["hidden"], t + 1)
                    if not whole or t >= GT:
                        at_least(act, S["hidT"], t - GT + 1)
                    A(hg[:, s, :], ps[:, 1 + s, :], ACT.Gelu).then_inc(S["gelu"], 1)

            schedule2(act, group)

        @block.vector
        def _(dve):
            V = nc.vector
            link = Chain(dve, S["dve"])
            V.memset(ones_f[:, :], 1.0).then_inc(S["ones_done"], 1)
            V.memset(ones_b[:, :], 1.0)
            V.memset(mh[:, :], -0.5)
            V.memset(g8[:, 19:20], 0.5)
            link(V.memset(seen[:, :, :], 0.0))
            V.memset(dn[:, 7, :], 0.0)
            V.memset(pad[:, 0:P + 1], 0.0)
            link(V.memset(pad[:, P + 1:ROW], float(2 * TOK)))
            V.tensor_copy(pad[:, P:P + 1], pad[:, 0:1]).then_inc(S["pad_ready"], 1)
            dve.wait_ge(S["consts_in"], 80)
            V.tensor_copy(x2[:, 0, :, P + 1], ids)
            V.tensor_scalar(x2[:, 1, :, P + 1], ids, float(UT), None, ALU.add)
            link(V.tensor_copy(before[:, :], before_f))
            dve.wait_ge(S["mix_rows"], 1)
            V.tensor_copy(dbc[:, :], W0[:, 0:96])
            V.tensor_copy(dlt[:, :], W1[0:RANK, 0:1]).then_inc(S["mix_rows_copied"], 1)
            dve.wait_ge(S["delta_raw"], 1)
            link(V.tensor_tensor(v[:, 0, :], W2[:, 0:2], sm[:, 0:2], ALU.add))
            link(V.tensor_scalar(v[:, 1, :], v[:, 0, :], -1.0, None, ALU.mult))
            V.tensor_tensor(v[:, 2, :], v[:, 0, :], v[:, 1, :], ALU.min).then_inc(S["delta_pre"], 1)
            dve.wait_ge(S["exp_a"], 1)
            V.tensor_scalar(v[:, 4, :], v[:, 3, :], 1.0, None, ALU.add).then_inc(S["exp_b"], 1)
            dve.wait_ge(S["ln_c"], 1)
            dve.wait_ge(S["exp_b"], 1)
            link(V.tensor_scalar(v[:, 6, :], v[:, 4, :], -1.0, None, ALU.add))
            V.tensor_scalar(v[:, 7, :], v[:, 6, :], 0.0, None, ALU.is_le)
            link(V.tensor_scalar(v[:, 8, :], v[:, 6, :], 1e-30, None, ALU.max))
            link(V.reciprocal(v[:, 9, :], v[:, 8, :]))
            link(V.tensor_tensor(v[:, 10, :], v[:, 9, :], v[:, 5, :], ALU.mult))
            link(V.tensor_tensor(v[:, 11, :], v[:, 10, :], v[:, 7, :], ALU.add))
            link(V.tensor_tensor(v[:, 12, :], v[:, 11, :], v[:, 3, :], ALU.mult))
            link(V.scalar_tensor_tensor(v[:, 13, :], v[:, 0, :], 0.0, v[:, 12, :], ALU.max, ALU.add))
            delta = v[:, 13, :].unsqueeze(2).to_broadcast([P, 2, NST])
            dve.wait_ge(S["act"], 1)
            dn3 = dn[:, :, :].rearrange("p k (c n) -> p k c n", c=2)
            link(V.tensor_tensor(dn3[:, 1], dn3[:, 0], delta, ALU.mult))
            V.tensor_scalar(dn[:, 2, :], dn[:, 1, :], -1.0, None, ALU.mult).then_inc(S["dax"], 1)
            link(V.tensor_tensor(dn[:, 4, 0:NST], dbc[:, RANK:RANK + NST], dbc[:, RANK + NST:96], ALU.mult))
            pw3 = pw[:, :, :].rearrange("p (c n) t -> p c n t", c=2)
            link(V.tensor_tensor(pw3[:, :, :, 0], dn[:, 4, 0:NST].unsqueeze(1).to_broadcast([P, 2, NST]), delta, ALU.mult))
            dve.wait_ge(S["exp_a"], 2)
            w, src = 1, 3
            while w < P:
                link(V.tensor_tensor(pw[:, :, w:2 * w], pw[:, :, 0:w],
                                     dn[:, src, :].unsqueeze(2).to_broadcast([P, 2 * NST, w]), ALU.mult))
                nxt = 8 - src if src != 3 else 5
                nxt = {3: 5, 5: 6, 6: 5}[src]
                if 2 * w < P:
                    link(V.tensor_tensor(dn[:, nxt, :], dn[:, src, :], dn[:, src, :], ALU.mult))
                w, src = 2 * w, nxt
            link(V.tensor_reduce(wsum[:, :, :], pw3.rearrange("p c n t -> p c t n"), AX.X, ALU.add))
            for c in range(2):
                last = V.tensor_tensor_scan(yd[:, c, :], wsum[:, c, :], pw[:, 0, :], 0.0, ALU.add, ALU.bypass)
            link(last)
            for c in range(2):
                last = V.tensor_scalar(yd[:, c, :], yd[:, c, :], sm[:, 2 + c:3 + c], 0.5, ALU.add, ALU.mult)
            last.then_inc(S["yd_ready"], 1)
            dve.wait_ge(S["weights_in"], 80)
            link(V.tensor_tensor(g8[:, 0:16], wgs[:, :], wgs[:, :], ALU.mult))
            V.tensor_reduce(g8[:, 16:17], g8[:, 0:16], AX.X, ALU.add).then_inc(S["router_norm"], 1)
            dve.wait_ge(S["router_pow"], 1)
            link(V.tensor_scalar(g8[:, 18:19], g8[:, 17:18], 1e-4, None, ALU.max))
            link(V.reciprocal(g8[:, 18:19], g8[:, 18:19]))
            V.tensor_scalar(g8[:, 0:16], wgs[:, :], g8[:, 18:19], None, ALU.mult).then_inc(S["router_norm"], 1)
            dve.wait_ge(S["wg_turned"], 1)
            V.tensor_copy(wgT[:, :], CT[0:16, 0:NE]).then_inc(S["wgT_ready"], 1)
            dve.wait_ge(S["router_mm"], 1)
            link(V.tensor_copy(wr[:, :], CT[:, 16:16 + NE]))
            dve.wait_ge(S["bias_in"], 16)
            for n in range(3):
                link(V.tensor_copy(bp[:, n, :], bf[:, n, :]))
                if n < 2:
                    link(V.tensor_tensor(bf[:, n + 1, :], bf[:, n, :], bp[:, n, :], ALU.subtract))
            V.tensor_copy(pr[:, 0, :], wr[:, :]).then_inc(S["bias_out"], 1)

            def variance(st, mv, ve, done):
                V.tensor_tensor(mv[:, 0], st[:, :, 1], st[:, :, 4], ALU.add)
                V.tensor_tensor(mv[:, 1], st[:, :, 1], st[:, :, 4], ALU.subtract)
                link(V.tensor_tensor(mv[:, 2], st[:, :, 2], st[:, :, 5], ALU.add))
                link(V.tensor_tensor(mv[:, 3], mv[:, 1], mv[:, 1], ALU.mult))
                link(V.scalar_tensor_tensor(mv[:, 4], mv[:, 2], 4.0 / P, mv[:, 3], ALU.mult, ALU.add))
                V.tensor_scalar(ve, mv[:, 4], 0.25, EPS, ALU.mult, ALU.add).then_inc(done, 1)

            def layer_norm(xs, st, mv, ve, done):
                for b in range(UB):
                    last = V.bn_stats(st[:, b, :], xs[:, b, :])
                link(last)
                variance(st, mv, ve[:, :], done)

            def unit(a, k, par, which):
                m, q, r, z = a + 1, a - 1, a - 2, a + 2
                att, mix, post, route = (runs(which, x) for x in (0, 1, -1, -2))
                mp = 1 - par
                W2r = W2[:, 0:UB * NE].rearrange("p (t e) -> p t e", t=UB)
                W2p = W2[:, UB * NE:2 * UB * NE].rearrange("p (t e) -> p t e", t=UB)

                def maximum(j):
                    i = UB * a + j
                    dve.wait_ge(S["scores"], i + 1)
                    at_least(dve, S["shifted"], i - 1)
                    V.tensor_reduce(mx[:, j % 2, :],
                                    ps[:, 2 * (j % 2):2 * (j % 2) + 2, :].rearrange("p g (h q) -> p q (g h)", h=4),
                                    AX.X, ALU.max).then_inc(S["max_ready"], 1)

                def inverse(j):
                    i = UB * a + j
                    jj, pp = (j - 1) % UB, (j - 1) % 2
                    dve.wait_ge(S["exp_ready"], i)
                    at_least(dve, S["attn_ready"], i - 2)
                    link(V.tensor_reduce(se[:, pp, :], E[:, jj, :, :].rearrange("p h q -> p q h"), AX.X, ALU.add))
                    V.reciprocal(re[:, pp, :], se[:, pp, :]).then_inc(S["recip_ready"], 1)

                if att:
                    maximum(0)
                if mix:
                    dve.wait_ge(S["mixed"], m + 1)
                    dve.wait_ge(xk_in[mp], 16 * ((k if par == 0 else k + 1) + 1))
                    at_least(dve, S["x1_ready"], m)
                    link(V.tensor_tensor(xs[:, :, :], W0.rearrange("p (b d) -> p b d", b=UB),
                                         xk[:, mp, :].rearrange("p (b d) -> p b d", b=UB), ALU.add))
                    layer_norm(xs, st, mv, ve, S["ln1_var"])
                if post:
                    inverse(0)
                if att:
                    maximum(1)
                if mix:
                    dve.wait_ge(S["ln1_rstd"], m + 1)
                    V.scalar_tensor_tensor(nb[:, :], mv[:, 0], -0.5, rs[:, :], ALU.mult,
                                           ALU.mult).then_inc(S["ln1_shift"], 1)
                if route:
                    dve.wait_ge(S["logits"], r + 1)
                    link(V.tensor_reduce(r4[:, 0, :], W2r, AX.X, ALU.max))
                    V.tensor_tensor(df[:, :, :], W2r, r4[:, 0, :].unsqueeze(2).to_broadcast([P, UB, NE]),
                                    ALU.subtract).then_inc(S["diff_ready"], 1)
                    dve.wait_ge(S["diff_ready"], r + 1)
                    link(V.scalar_tensor_tensor(rk[:, :, :].rearrange("p t e -> p (t e)"),
                                                df[:, :, :].rearrange("p t e -> p (t e)"), 0.0, rank,
                                                ALU.is_ge, ALU.mult))
                    link(V.tensor_reduce(r4[:, 1, :], rk[:, :, :], AX.X, ALU.max))
                    link(V.tensor_tensor(oh[:, :, :], rank.rearrange("p (t e) -> p t e", t=UB),
                                         r4[:, 1, :].unsqueeze(2).to_broadcast([P, UB, NE]), ALU.is_equal))
                    V.tensor_reduce(cu[:, :], oh[:, :, :].rearrange("p t e -> p e t"), AX.X,
                                    ALU.add).then_inc(S["onehot"], 1)
                if att:
                    inverse(1)
                if att:
                    maximum(2)
                    inverse(2)
                if route:
                    dve.wait_ge(S["onehot"], r + 1)
                    at_least(dve, S["pos_ready"], r)
                    V.tensor_tensor(seen[:, par, :], seen[:, mp, :], cu[:, :], ALU.add)
                    dve.wait_ge(S["pos_ready"], r + 1)
                    link(V.tensor_tensor(pr[:, :, :], W2p, oh[:, :, :], ALU.mult))
                    link(V.tensor_reduce(r4[:, 2, :], pr[:, :, :], AX.X, ALU.add))
                    link(V.scalar_tensor_tensor(r4[:, 3, :], r4[:, 1, :], float(-CAP), r4[:, 2, :],
                                                ALU.mult, ALU.add))
                    dve.wait_ge(S["gate_exp"], r + 1)
                    link(V.tensor_reduce(r4[:, 4, :], er[:, :, :], AX.X, ALU.add))
                    V.reciprocal(x2[:, par, :, P], r4[:, 4, :])
                    link(V.tensor_scalar(x2[:, par, :, P + 1], x2[:, par, :, P + 1], float(2 * UT), None, ALU.add))
                    V.tensor_scalar(idx[:, par, :], r4[:, 3, :], float(NE * CAP), None,
                                    ALU.add).then_inc(S["idx_ready"], 1)
                if post:
                    dve.wait_ge(S["proj"], q + 1)
                    at_least(dve, S["x2_ready"], q)
                    dve.wait_ge(S["x1_kept"], q + 1)
                    V.tensor_tensor(xs2[:, :, :], W1.rearrange("p (b d) -> p b d", b=UB),
                                    x1r[:, mp, :, :], ALU.add).then_inc(S["ln2_sum"], 1)
                    dve.wait_ge(S["ln2_sum"], q + 1)
                    layer_norm(xs2, st2, mv2, ve2, S["ln2_var"])
                if att:
                    maximum(3)
                    inverse(3)
                if post:
                    dve.wait_ge(S["ln2_rstd"], q + 1)
                    V.scalar_tensor_tensor(nb2[:, :], mv2[:, 0], -0.5, rs2[:, :], ALU.mult,
                                           ALU.mult).then_inc(S["ln2_shift"], 1)
                if runs(which, 2):
                    dve.wait_ge(S["tanh_ready"], z + 1)
                    at_least(dve, S["g_ready"], z)
                    V.scalar_tensor_tensor(th[:, :, :], th[:, :, :], 1.0, ps[:, 4:6, :], ALU.add,
                                           ALU.mult).then_inc(S["u_ready"], 1)

            schedule(dve, unit, link, VECTOR_STEPS)

            dve.wait_ge(S["counts"], 1)
            link(V.tensor_copy(cn[:, 0, :], W0[:, 0:NE]))
            link(V.tensor_scalar(cn[:, 1, :], cst[:, 3 * P + H:3 * P + H + NE], float(-CAP),
                                 float(NE * CAP), ALU.mult, ALU.add))
            link(V.tensor_tensor(cn[:, 2, :], cn[:, 1, :], cn[:, 0, :], ALU.add))
            V.tensor_scalar(pidx[:, :], cn[:, 2, :], cst[:, 3 * P + H + UB * NE:3 * P + H + UB * NE + 1],
                            float(2 * UT), ALU.add, ALU.add).then_inc(S["counts"], 1)
            link(V.tensor_scalar(cn[0:1, 3, :], cn[0:1, 0, :], float(P - 1), 1.0 / P, ALU.add, ALU.mult))
            link(V.tensor_scalar(cni[:, :], cn[0:1, 3, :], 1.0 / 256 - 0.5, None, ALU.add))
            link(V.tensor_copy(cn[0:1, 4, :], cni[:, :]))
            link(V.tensor_tensor_scan(cn[0:1, 5, :], cn[0:1, 4, :], cn[0:1, 4, :], 0.0, ALU.add, ALU.bypass))
            g3 = ge[:, :, :].rearrange("p k (t e) -> p k t e", e=NE)
            link(V.tensor_tensor(g3[:, 0], tnum.rearrange("p (t e) -> p t e", e=NE),
                                 cn[0:1, 5, :].unsqueeze(1).to_broadcast([1, NT, NE]), ALU.is_ge))
            link(V.tensor_reduce(tb[:, 0, :], g3[:, 0], AX.X, ALU.add))
            link(V.tensor_tensor(g3[:, 1], g3[:, 0],
                                 cn[0:1, 4, :].unsqueeze(1).to_broadcast([1, NT, NE]), ALU.mult))
            link(V.tensor_reduce(tb[:, 1, :], g3[:, 1], AX.X, ALU.add))
            link(V.tensor_tensor(tb[:, 2, :], tnum.rearrange("p (t e) -> p t e", e=NE)[:, :, 0], tb[:, 1, :], ALU.subtract))
            link(V.tensor_scalar(tb[:, 3, :], tb[:, 0, :], float(CAP), None, ALU.mult))
            link(V.scalar_tensor_tensor(tb[:, 4, :], tb[:, 2, :], float(P), tb[:, 3, :], ALU.mult, ALU.add))
            link(V.tensor_scalar(tab[:, 0, :], tb[:, 4, :], float(NE * CAP), None, ALU.min))
            V.tensor_scalar(tab[:, 1, :], tb[:, 0, :], float(NE - 1), None, ALU.min).then_inc(S["table_ready"], 1)

            def group(n, k, par):
                whole = isinstance(n, int)
                for s in range(GT):
                    t = n * GT + s
                    if s == 0 and (not whole or n >= 2):
                        dve.wait_ge(S["rstd3"], n - 1)
                        lo, hi = par * GT, par * GT + GT
                        V.scalar_tensor_tensor(nb3[:, lo:hi], mv3[:, 0, lo:hi], -0.5, rs3[:, lo:hi],
                                               ALU.mult, ALU.mult).then_inc(S["shift3"], 1)
                    if not whole or 1 <= t < NT + 1:
                        sb_ = (s - 1) % GT
                        dve.wait_ge(S["hidT"], t)
                        if not whole or t - 1 >= GT:
                            at_least(dve, S["y_ready"], t - GT)
                        V.tensor_copy(hT[:, sb_, :], ps[:, 4 + sb_, :]).then_inc(S["hidT_copied"], 1)
                    if not whole or 2 <= t < NT + 2:
                        slot = (par * GT + s - 2) % NX
                        kk = k if s == 2 or par == 1 else k - 1
                        dve.wait_ge(S["y_ready"], t - 1)
                        if not whole or t - 2 >= NX:
                            at_least(dve, S["out_ready"], t - 2 - NX + 1)
                            dve.wait_ge(final_out[slot], 16 * kk)
                        link(V.tensor_copy(tix[:, slot:slot + 1], xr[:, slot, P + 1:ROW]))
                        V.scalar_tensor_tensor(rsd[:, slot, :], ps[:, 7, 0:P], xr[:, slot, P:P + 1],
                                               xr[:, slot, 0:P], ALU.mult, ALU.add).then_inc(S["res_ready"], 1)
                        dve.wait_ge(S["res_ready"], t - 1)
                        link(V.bn_stats(st3[:, slot, :], rsd[:, slot, :]))
                    if s == 1 and (not whole or 1 <= n <= NG):
                        lo = (1 - par) * GT
                        variance(st3[:, lo:lo + GT, :], mv3[:, :, lo:lo + GT], ve3[:, lo:lo + GT], S["var3"])

            schedule2(dve, group, link, VECTOR_STEPS_2)

        @block.gpsimd
        def _(pool):
            G = nc.gpsimd
            G.memset(vbd[:, 0, :, :], 0.0)
            G.memset(vbd[:, 1, :, :], 0.0)
            G.memset(bias[:, :], 0.0)
            G.memset(ones3[:, :], 0.0).then_inc(S["memset_done"], 1)
            pool.wait_ge(S["memset_done"], 1)
            G.memset(ones3[0:3, :], 1.0).then_inc(S["memset_done"], 1)
            G.iota(tailx[:, :], pattern=[[QR, UB]], base=NE * CAP, channel_multiplier=1).then_inc(S["memset_done"], 1)
            pool.wait_ge(S["pad_ready"], 1)
            pool.wait_ge(S["memset_done"], 3)
            for t in range(UB):
                G.indirect_dma_start(out=lists, out_offset=bass.IndirectOffsetOnAxis(ap=tailx[:, t:t + 1], axis=0),
                                     in_=pad[0:QR, :], in_offset=None).then_inc(rows_out[UB + t], 16)
            pool.wait_ge(S["router_norm"], 1)
            G.tensor_tensor(g8[:, 17:18], g8[:, 16:17], g8[:, 19:20], ALU.pow).then_inc(S["router_pow"], 1)

            def unit(a, k, par, which):
                m, q, r, z = a + 1, a - 1, a - 2, a + 2
                att, mix, post, route = (runs(which, x) for x in (0, 1, -1, -2))
                mp = 1 - par

                def normalize(j):
                    i = UB * a + j
                    jj, pp = (j - 1) % UB, (j - 1) % 2
                    pool.wait_ge(S["recip_ready"], i)
                    G.tensor_tensor(E[:, jj, :, :], E[:, jj, :, :],
                                    re[:, pp, :].unsqueeze(1).to_broadcast([P, H, P]),
                                    ALU.mult).then_inc(S["attn_ready"], 1)

                if mix:
                    pool.wait_ge(S["ln1_var"], m + 1)
                    at_least(pool, S["x1_ready"], m)
                    G.tensor_tensor(rs[:, :], ve[:, :], mh[:, :], ALU.pow).then_inc(S["ln1_rstd"], 1)
                if post:
                    normalize(0)
                if att:
                    normalize(1)
                    normalize(2)
                if post:
                    pool.wait_ge(S["ln2_var"], q + 1)
                    at_least(pool, S["x2_ready"], q)
                    G.tensor_tensor(rs2[:, :], ve2[:, :], mh[:, :], ALU.pow).then_inc(S["ln2_rstd"], 1)
                if mix:
                    wait_apart(pool, S["x1_ready"], m + 1, S["ones_done"])
                    if post:
                        pool.wait_ge(S["ln2_sum"], q + 1)
                    G.tensor_copy(x1r[:, mp, :, :], x1[:, :, :]).then_inc(S["x1_kept"], 1)
                if route:
                    wait_apart(pool, S["idx_ready"], r + 1, S["ones_done"])
                    for t in range(UB):
                        G.indirect_dma_start(
                            out=lists, out_offset=bass.IndirectOffsetOnAxis(ap=idx[:, par, t:t + 1], axis=0),
                            in_=x2[:, par, t, :], in_offset=None).then_inc(rows_out[par * UB + t], 16)
                if att:
                    normalize(3)
                if runs(which, 2):
                    pool.wait_ge(S["u_ready"], z + 1)
                    at_least(pool, S["mixed"], z)
                    if which[0] == -2:
                        pool.wait_ge(S["yd_ready"], 1)
                    for c in range(2):
                        last = G.tensor_tensor(g[:, c, :].rearrange("p (b l) -> p b l", b=UB),
                                               th[:, c, :].rearrange("p (b l) -> p b l", b=UB),
                                               yd[:, c, :].unsqueeze(1).to_broadcast([P, UB, P]), ALU.mult)
                    last.then_inc(S["g_ready"], 1)

            schedule(pool, unit)

            pool.wait_ge(S["counts"], 2)
            for e in range(NE):
                G.indirect_dma_start(out=lists, out_offset=bass.IndirectOffsetOnAxis(ap=pidx[:, e:e + 1], axis=0),
                                     in_=pad[:, :], in_offset=None).then_inc(S["pads_out"], 16)

            def group(n, k, par):
                whole = isinstance(n, int)
                if not whole or 1 <= n <= NG:
                    lo = (1 - par) * GT
                    pool.wait_ge(S["var3"], n)
                    if not whole or 2 <= n:
                        pool.wait_ge(S["out_ready"], (n - 1) * GT)
                    G.tensor_tensor(rs3[:, lo:lo + GT], ve3[:, lo:lo + GT], mh[:, 0:GT],
                                    ALU.pow).then_inc(S["rstd3"], 1)
                if not whole or 2 <= n:
                    if whole and n > NG:
                        pool.wait_ge(S["out_ready"], (n - 1) * GT)
                    for s in range(GT):
                        slot = par * GT + s
                        G.indirect_dma_start(
                            out=out, out_offset=bass.IndirectOffsetOnAxis(ap=tix[:, slot:slot + 1], axis=0),
                            in_=ot[:, slot, :], in_offset=None, bounds_check=TOK - 1,
                            oob_is_err=False).then_inc(final_out[slot], 16)

            schedule2(pool, group)
            for slot in range(NX):
                pool.wait_ge(final_out[slot], 16 * ((NG + (slot < GT)) // 2))
            for n, q in enumerate(rows_out):
                pool.wait_ge(q, 16 * (UN // 2 + n // UB))
            pool.wait_ge(S["pads_out"], 16 * NE)
            pool.wait_ge(S["bias_back"], 32)


VECTOR_STEPS = 44
VECTOR_STEPS_2 = 18


def constants():
    f = np.float32
    p = np.arange(P)
    hmask = (p[:, None] // DH == np.arange(H)[None, :]).astype(f) * f(DH ** -0.5)
    rank = np.tile(NE - np.arange(NE), UB)[None, :].repeat(P, 0).astype(f)
    ids = (p[:, None] + P * np.arange(UB)[None, :] - 2 * UT).astype(f)
    tnum = np.repeat(np.arange(NT), NE)[None, :].repeat(P, 0).astype(f)
    before = (p[:, None] < p[None, :]).astype(f)
    rest = np.zeros((P, 4), f)
    rest[:, 0], rest[:, 1] = 1.0, -0.5
    return np.ascontiguousarray(np.concatenate(
        [np.eye(P, dtype=f), -np.eye(P, dtype=f), before, hmask, rank, ids, tnum, rest], 1))


def kernel(x, ctx_1024, L0_attn_W_in, L0_attn_conv_w, L0_attn_conv_b, L0_attn_W_x, L0_attn_W_dt,
           L0_attn_b_dt, L0_attn_A_log, L0_attn_D_skip, L0_attn_W_out, L0_xattn_W_Q, L0_xattn_W_K,
           L0_xattn_W_V, L0_xattn_W_O, L0_ffn_w_red, L0_ffn_wg, L0_ffn_w1, L0_ffn_b1, L0_ffn_w2, L0_ffn_b2):
    import concourse.bacc as bacc
    from concourse.bass_utils import run_bass_kernel_spmd

    def c(a):
        return np.ascontiguousarray(a)

    x, ctx_1024 = np.asarray(x), np.asarray(ctx_1024)
    chunks = lambda a: c(np.asarray(a).reshape(2, P, -1).transpose(1, 0, 2))
    t = lambda a: np.asarray(a).T
    w1, w2 = np.asarray(L0_ffn_w1), np.asarray(L0_ffn_w2)
    ins = {
        "x_t": c(x.transpose(2, 0, 1).reshape(P, TOK)),
        "x_tok": c(x.transpose(1, 0, 2).reshape(P, TOK)),
        "ctx_t": c(ctx_1024.transpose(2, 0, 1).reshape(P, TOK)),
        "wz_t": c(t(L0_attn_W_in)[:, EI:]),
        "wx_t": chunks(t(L0_attn_W_x)),
        "wdt_t": c(t(L0_attn_W_dt)),
        "small": c(np.concatenate([np.asarray(L0_attn_b_dt).reshape(2, P).T,
                                   np.asarray(L0_attn_D_skip).reshape(2, P).T], 1)),
        "a_log": chunks(L0_attn_A_log),
        "wout_t": chunks(t(L0_attn_W_out)),
        "wqkvo_t": c(np.stack([t(L0_xattn_W_Q), t(L0_xattn_W_K), t(L0_xattn_W_V), t(L0_xattn_W_O)], 1)),
        "wred_t": c(t(L0_ffn_w_red)),
        "wg": c(np.asarray(L0_ffn_wg)),
        "w1": c(w1.transpose(1, 0, 2).reshape(P, NE * FF)),
        "w2": c(w2.reshape(NE, FC, P, P).transpose(2, 0, 1, 3).reshape(P, NE * FC * P)),
        "b12": c(np.concatenate([np.asarray(L0_ffn_b1).reshape(-1), np.asarray(L0_ffn_b2).reshape(-1)]).reshape(P, -1)),
        "consts": constants(),
    }
    nc = bacc.Bacc("TRN2", target_bir_lowering=False, num_devices=1)
    args = [nc.dram_tensor("in_" + n, a.shape, mybir.dt.from_np(a.dtype), kind="ExternalInput").ap()
            for n, a in ins.items()]
    out = nc.dram_tensor("out", [TOK, P], F32, kind="ExternalOutput").ap()
    decoder_program(nc, *args, out)
    r = run_bass_kernel_spmd(nc, [{"in_" + n: a for n, a in ins.items()}], core_ids=[0])
    return r.results[0]["out"].reshape(NSEQ, P, P)
```

```python
from contextlib import ExitStack

import numpy as np

import concourse.bass as bass
from concourse import mybir

ALU = mybir.AluOpType
ACT = mybir.ActivationFunctionType
AX = mybir.AxisListType
F32 = mybir.dt.float32
BF16 = mybir.dt.bfloat16
I32 = mybir.dt.int32
U32 = mybir.dt.uint32

P = 128
NSEQ = 32
UB = 4
UN = NSEQ // UB
UT = UB * P
H, DH = 8, 16
EI, NST, RANK = 256, 16, 64
NE, FF = 8, 512
FC = FF // P
TOK = NSEQ * P
CAP = TOK + P
ROW = P + 2
NT = TOK // P + NE - 1
GT = 3
NG = NT // GT
QR = P // UB
EPS = 1e-5


def at_least(eng, sem, n):
    if isinstance(n, int) and n <= 0:
        return
    eng.wait_ge(sem, n)


class Chain:

    def __init__(self, eng, sem):
        self.eng, self.sem, self.done, self.n = eng, sem, 0, 0

    def __call__(self, ins):
        self.n += 1
        ins.then_inc(self.sem, 1)
        self.eng.wait_ge(self.sem, self.done + self.n)

    def enter(self, rounds, per_round):
        self.before, self.per_round = self.done + self.n, per_round
        self.done, self.n = self.before + rounds * per_round, 0

    def leave(self, rounds):
        assert self.n == self.per_round, f"a round has {self.n} steps"
        self.done, self.n = self.before + rounds * self.per_round, 0


def decoder_program(nc, x_t, x_tok, ctx_t, wz_t, wx_t, wdt_t, small, a_log, wout_t, wqkvo_t,
                    wred_t, wg, w1, w2, b12, consts, out):
    ctx = ExitStack()
    with ctx:
        def sb(name, shape, dt=F32):
            return ctx.enter_context(nc.sbuf_tensor(name, shape, dt))

        def sem(name):
            return ctx.enter_context(nc.semaphore(name))

        lists = nc.dram_tensor("expert_lists", [(NE + 1) * CAP, ROW], F32, kind="Internal").ap()
        bias_parts = nc.dram_tensor("bias_parts", [3, NE * (FF + P)], BF16, kind="Internal").ap()

        ps = ctx.enter_context(nc.psum_tensor("ps", [P, 8, 512], F32))
        W0, W1, W2, CT = ps[:, 4, :], ps[:, 5, :], ps[:, 6, :], ps[:, 7, :]

        wz = sb("wz", [P, EI]); wx = sb("wx", [P, 2, 96]); wdt = sb("wdt", [RANK, EI])
        sm = sb("sm", [P, 4])
        alog = sb("alog", [P, 2, NST]); wout = sb("wout", [P, 2, P])
        wqkvo = sb("wqkvo", [P, 4, P]); wred = sb("wred", [16, P]); wgs = sb("wgs", [NE, 16])
        w1s = sb("w1s", [P, NE * FF]); w2s = sb("w2s", [P, NE * FC * P])
        CW = 2 * P + 8 + 32 + 4 + 39 * 8 + 4
        cst = sb("cst", [P, CW])
        o = 0
        ident = cst[:, o:o + P]; o += P
        before_f = cst[:, o:o + P]; o += P
        hmask = cst[:, o:o + H]; o += H
        rank = cst[:, o:o + UB * NE]; o += UB * NE
        ids = cst[:, o:o + UB]; o += UB
        tnum = cst[0:1, o:o + NT * NE]; o += NT * NE
        ones_c = cst[:, o:o + 1]; mhalf = cst[:, o + 1:o + 2]; o += 4

        ones_b = sb("ones_b", [P, P], BF16); before = sb("before", [P, P], BF16)
        ones3 = sb("ones3", [P, P], BF16)
        ones_f = sb("ones_f", [P, P])
        mh = sb("mh", [P, 4])

        dbc = sb("dbc", [P, 96]); dlt = sb("dlt", [RANK, 1])
        v = sb("v", [P, 14, 2]); dn = sb("dn", [P, 8, 2 * NST])
        yd = sb("yd", [P, 2, P]); wsum = sb("wsum", [P, 2, P])
        wr = sb("wr", [P, NE]); g8 = sb("g8", [NE, 20]); wgT = sb("wgT", [16, NE])
        xt = sb("xt", [P, 2, UT]); xk = sb("xk", [P, 2, UT]); ct_in = sb("ct_in", [P, 2, UT])
        th = sb("th", [P, 2, UT]); g = sb("g", [P, 2, UT])
        xs = sb("xs", [P, UB, P]); st = sb("st", [P, UB, 6]); mv = sb("mv", [P, 5, UB])
        ve = sb("ve", [P, UB]); rs = sb("rs", [P, UB]); nb = sb("nb", [P, UB])
        xs2 = sb("xs2", [P, UB, P]); st2 = sb("st2", [P, UB, 6]); mv2 = sb("mv2", [P, 5, UB])
        ve2 = sb("ve2", [P, UB]); rs2 = sb("rs2", [P, UB]); nb2 = sb("nb2", [P, UB])
        x1 = sb("x1", [P, UB, P]); x1r = sb("x1r", [P, 2, UB, P]); x1T = sb("x1T", [P, UT])
        qbd = sb("qbd", [P, 2, H, UB, P]); kt = sb("kt", [P, UB, P])
        VW = H * (P + DH)
        vbd = sb("vbd", [P, 2, UB, VW])
        mx = sb("mx", [P, P]); E = sb("E", [P, 4, H, P]); se = sb("se", [P, 2, P])
        pw = E[:, :, :, :].rearrange("p j h q -> p (j h) q")
        re = sb("re", [P, 2, P]); ctT = sb("ctT", [P, UB, P])
        x2 = sb("x2", [P, 2, UB, ROW]); x2T = sb("x2T", [P, UB, P])
        df = sb("df", [P, UB, NE]); er = sb("er", [P, UB, NE]); rk = sb("rk", [P, UB, NE])
        r4 = sb("r4", [P, 6, UB]); oh = sb("oh", [P, UB, NE], BF16)
        seen = sb("seen", [P, 2, NE], BF16); cu = sb("cu", [P, NE]); pr = sb("pr", [P, UB, NE])
        idx = sb("idx", [P, 2, UB], U32)
        pad = sb("pad", [P, ROW]); tailx = sb("tailx", [QR, UB], U32)
        tb = sb("tb", [1, 12, NT]); cn = sb("cn", [P, 8, NE]); cni = sb("cni", [1, NE], I32)
        ge = sb("ge", [1, 2, NT * NE]); tab = sb("tab", [1, 2, NT], I32); pidx = sb("pidx", [P, NE], U32)
        BW = NE * (FF + P) // P
        bf = sb("bf", [P, 3, BW]); bp = sb("bp", [P, 3, BW], BF16)
        bias = sb("bias", [P, NE * (FF + P)], BF16)
        NX = 2 * GT
        xr = sb("xr", [P, NX, ROW]); xrT = sb("xrT", [P, GT, P])
        q0 = qbd[:, 0, :, :, :].rearrange("p h b q -> p (h b q)")
        q1 = qbd[:, 1, :, :, :].rearrange("p h b q -> p (h b q)")
        hg = q0[:, 0:GT * FF].rearrange("p (s f) -> p s f", s=GT)
        hT = q0[:, GT * FF:2 * GT * FF].rearrange("p (s f) -> p s f", s=GT)
        rsd = q1[:, 0:NX * P].rearrange("p (s f) -> p s f", s=NX)
        ot = q1[:, NX * P:2 * NX * P].rearrange("p (s f) -> p s f", s=NX)
        tix = sb("tix", [P, NX], U32)
        st3 = sb("st3", [P, NX, 6]); mv3 = sb("mv3", [P, 5, NX])
        ve3 = sb("ve3", [P, NX]); rs3 = sb("rs3", [P, NX]); nb3 = sb("nb3", [P, NX])

        S = {n: sem(n) for n in (
            "consts_in weights_in experts_in bias_in bias_out bias_back memset_done ones_done mix_rows mix_rows_copied "
            "delta_pre delta_raw exp_a exp_b ln_c dax yd_ready router_norm router_pow wg_turned wgT_ready "
            "router_mm wr_ready "
            "z_ready tanh_ready u_ready g_ready mixed ln1_var ln1_rstd ln1_shift x1_ready x1_kept x1T_ready "
            "x1T_copied q_ready qbd_ready k_ready k_copied v_ready v_copied "
            "scores  shifted exp_ready recip_ready attn_ready ctx_ready ctx_copied "
            "proj ln2_sum ln2_var ln2_rstd ln2_shift x2_ready x2T_ready x2T_copied logits diff_ready "
            "gate_exp onehot pos_ready idx_ready pads_out pad_ready counts table_ready "
            "dve act pool rowT rowT_copied hidden gelu hidT hidT_copied y_ready res_ready var3 rstd3 "
            "shift3 out_ready tix_ready").split()}
        xt_in = [sem(f"xt_in{p}") for p in range(2)]
        xk_in = [sem(f"xk_in{p}") for p in range(2)]
        ct_in_s = [sem(f"ctx_in{p}") for p in range(2)]
        rows_out = [sem(f"rows_out{k}") for k in range(2 * UB)]
        rows_in = [sem(f"rows_in{k}") for k in range(NX)]
        final_out = [sem(f"final_out{k}") for k in range(NX)]

        def schedule(eng, unit, chain=None, per_round=0):
            for a in (-2, -1, 0, 1):
                unit(a, a // 2, a % 2, range(a, a + 1))
            with eng.Fori(1, 3) as k:
                if chain:
                    chain.enter(k - 1, per_round)
                unit(2 * k, k, 0, range(2, 5))
                unit(2 * k + 1, k, 1, range(3, 6))
                if chain:
                    chain.leave(2)
            for a in (6, 7, 8, 9):
                unit(a, a // 2, a % 2, range(a, a + 1))

        def runs(which, shift):
            return 0 <= which[0] + shift < UN

        def schedule2(eng, group, chain=None, per_round=0):
            for n in range(5):
                group(n, n // 2, n % 2)
            with eng.Fori(2, NG // 2 - 1) as k:
                if chain:
                    chain.enter(k - 2, per_round)
                group(2 * k + 1, k, 1)
                group(2 * k + 2, k + 1, 0)
                if chain:
                    chain.leave(NG // 2 - 3)
            for n in range(NG - 2, NG + 2):
                group(n, n // 2, n % 2)

        block = ctx.enter_context(nc.Block())

        @block.sync
        def _(sp):
            def load(n, par):
                cols = bass.ds(n * UT, UT)
                at_least(sp, S["z_ready"], n - 1 if not isinstance(n, int) or n > 1 else 0)
                sp.dma_start(xt[:, par, :], x_t[:, cols]).then_inc(xt_in[par], 16)
                at_least(sp, S["ln1_var"], n - 1 if not isinstance(n, int) or n > 1 else 0)
                sp.dma_start(xk[:, par, :], x_tok[:, cols]).then_inc(xk_in[par], 16)
                at_least(sp, S["v_ready"], n - 1 if not isinstance(n, int) or n > 1 else 0)
                sp.dma_start(ct_in[:, par, :], ctx_t[:, cols]).then_inc(ct_in_s[par], 16)

            sp.dma_start(wx[:, :, :], wx_t).then_inc(S["consts_in"], 16)
            sp.dma_start(wdt[:, :], wdt_t).then_inc(S["consts_in"], 16)
            sp.dma_start(sm[:, :], small).then_inc(S["consts_in"], 16)
            sp.dma_start(alog[:, :, :], a_log).then_inc(S["consts_in"], 16)
            sp.dma_start(cst[:, :], consts).then_inc(S["consts_in"], 16)
            sp.dma_start(wz[:, :], wz_t).then_inc(S["weights_in"], 16)
            load(0, 0)
            sp.dma_start(wout[:, :, :], wout_t).then_inc(S["weights_in"], 16)
            sp.dma_start(wqkvo[:, :, :], wqkvo_t).then_inc(S["weights_in"], 16)
            sp.dma_start(wred[:, :], wred_t).then_inc(S["weights_in"], 16)
            sp.dma_start(wgs[:, :], wg).then_inc(S["weights_in"], 16)
            load(1, 1)
            sp.dma_start(bf[:, 0, :], b12).then_inc(S["bias_in"], 16)
            sp.dma_start(w1s[:, :], w1).then_inc(S["experts_in"], 16)
            sp.dma_start(w2s[:, :], w2).then_inc(S["experts_in"], 16)
            sp.wait_ge(S["bias_out"], 1)
            sp.dma_start(bias_parts.rearrange("k (p f) -> p k f", p=P), bp[:, :, :]).then_inc(S["bias_back"], 16)
            sp.wait_ge(S["bias_back"], 16)
            sp.dma_start(bias[0:3, :], bias_parts).then_inc(S["bias_back"], 16)
            with sp.Fori(1, UN // 2) as k:
                load(2 * k, 0)
                load(2 * k + 1, 1)

            sp.wait_ge(S["table_ready"], 1)
            for n, q in enumerate(rows_out):
                sp.wait_ge(q, 16 * (UN // 2 + n // UB))
            sp.wait_ge(S["pads_out"], 16 * NE)

            def group(n, k, par):
                if isinstance(n, int) and n >= NG:
                    return
                for s in range(GT):
                    t = n * GT + s
                    slot = par * GT + s
                    if not (isinstance(n, int) and n < 2):
                        at_least(sp, S["res_ready"], t - NX + 1)
                    at = sp.value_load(tab[0:1, 0, bass.ds(t, 1)], min_val=0, max_val=NE * CAP)
                    sp.dma_start(xr[:, slot, :], lists[bass.ds(at, P), :]).then_inc(rows_in[slot], 16)

            group(0, 0, 0)
            group(1, 0, 1)
            with sp.Fori(1, (NG + 1) // 2 - 1) as k:
                group(2 * k, k, 0)
                group(2 * k + 1, k, 1)
            group(NG - 1, NG // 2, 0)

        @block.tensor
        def _(pe):
            mm, tr = nc.tensor.matmul, nc.tensor.transpose
            pe.wait_ge(S["consts_in"], 80)
            pe.wait_ge(S["ones_done"], 1)
            for c in range(2):
                mm(W0[:, 0:96], ones_f[:, :], wx[:, c, :], start=(c == 0), stop=(c == 1))
            for c in range(2):
                last = mm(W1[0:RANK, 0:1], wx[:, c, 0:RANK], ones_f[:, 0:1], start=(c == 0), stop=(c == 1))
            last.then_inc(S["mix_rows"], 1)
            pe.wait_ge(S["mix_rows_copied"], 1)
            for c in range(2):
                last = mm(W2[:, c:c + 1], wdt[:, c * P:(c + 1) * P], dlt[:, :], start=True, stop=True)
            last.then_inc(S["delta_raw"], 1)
            pe.wait_ge(S["router_norm"], 2)
            pe.wait_ge(S["weights_in"], 80)
            tr(CT[0:16, 0:NE], g8[:, 0:16], ident[0:NE, 0:NE]).then_inc(S["wg_turned"], 1)
            pe.wait_ge(S["wgT_ready"], 1)
            mm(CT[:, 16:16 + NE], wred[:, :], wgT[:, :], start=True, stop=True).then_inc(S["router_mm"], 1)

            def unit(a, k, par, which):
                z, m, q, r = a + 2, a + 1, a - 1, a - 2
                gate, mix, att, post, route = (runs(which, x) for x in (2, 1, 0, -1, -2))
                mp = 1 - par

                def score(i, first):
                    jj = first % UB
                    pp = par if first < UB else mp
                    if first == UB:
                        pe.wait_ge(S["qbd_ready"], m + 1)
                        pe.wait_ge(S["k_copied"], m + 1)
                    at_least(pe, S["shifted"], i - 1)
                    for hh in range(2):
                        last = mm(ps[:, 2 * (jj % 2) + hh, :], kt[:, jj, :],
                                  qbd[:, pp, 4 * hh:4 * hh + 4, jj, :], start=True, stop=True)
                    last.then_inc(S["scores"], 1)

                def context(j):
                    jj, vp = (j - 2) % UB, par if j >= 2 else mp
                    pe.wait_ge(S["attn_ready"], UB * a + j - 1)
                    if j == 2:
                        pe.wait_ge(S["v_copied"], a + 1)
                        at_least(pe, S["ctx_copied"], a)
                    for h in range(H):
                        last = mm(CT[:, jj * P:(jj + 1) * P], vbd[:, vp, jj, h * P:(h + 1) * P],
                                  E[:, jj, h, :], start=(h == 0), stop=(h == H - 1))
                    last.then_inc(S["ctx_ready"], 1)

                if route:
                    pe.wait_ge(S["onehot"], r + 1)
                    pe.wait_ge(S["ln2_sum"], r + 1)
                    pe.wait_ge(S["qbd_ready"], a + 1 if att else UN)
                    kw = dict(skip_group_check=True)
                    pos = W2[:, UB * NE:2 * UB * NE]
                    mm(pos, before[:, :], oh[:, :, :], start=True, stop=False, **kw)
                    mm(pos, ones_b[:, :], seen[:, mp, :].unsqueeze(1).to_broadcast([P, UB, NE]),
                       start=False, stop=False, **kw)
                    for t in range(1, UB):
                        last = mm(pos[:, t * NE:], ones_b[:, :], oh[:, 0:UB - t, :],
                                  start=False, stop=(t == UB - 1), **kw)
                    last.then_inc(S["pos_ready"], 1)
                if att:
                    score(UB * a + 1, 1)
                if gate:
                    pe.wait_ge(xt_in[par], (k + 2) * 16)
                    at_least(pe, S["ln1_var"], z)
                    if route:
                        pe.wait_ge(S["diff_ready"], r + 1)
                    if att:
                        pe.wait_ge(S["k_copied"], a + 1)
                    mm(W0, wz[:, 0:P], xt[:, par, :], start=True, stop=True)
                    mm(W1, wz[:, P:2 * P], xt[:, par, :], start=True, stop=True).then_inc(S["z_ready"], 1)
                if post:
                    context(0)
                if mix:
                    pe.wait_ge(S["x1_ready"], m + 1)
                    if gate:
                        pe.wait_ge(S["u_ready"], z + 1)
                    elif att:
                        pe.wait_ge(S["k_copied"], a + 1)
                    for b in range(UB):
                        last = tr(W1[:, b * P:(b + 1) * P], x1[:, b, :], ident)
                    last.then_inc(S["x1T_ready"], 1)
                if att:
                    score(UB * a + 2, 2)
                if post:
                    context(1)
                    pe.wait_ge(S["ctx_copied"], q + 1)
                    if route:
                        pe.wait_ge(S["idx_ready"], r + 1)
                    if att:
                        pe.wait_ge(S["qbd_ready"], a + 1)
                    at_least(pe, S["ln2_sum"], q)
                    for b in range(UB):
                        last = mm(W2[:, b * P:(b + 1) * P], ctT[:, b, :], wqkvo[:, 3, :],
                                  start=True, stop=True)
                    last.then_inc(S["proj"], 1)
                if att:
                    pe.wait_ge(ct_in_s[par], (k + 1) * 16)
                    if mix:
                        pe.wait_ge(S["x1T_copied"], m + 1)
                    for b in range(UB):
                        last = mm(W1[:, b * P:(b + 1) * P], ct_in[:, par, b * P:(b + 1) * P],
                                  wqkvo[:, 2, :], start=True, stop=True)
                    last.then_inc(S["v_ready"], 1)
                if gate:
                    pe.wait_ge(S["g_ready"], z + 1)
                    for b in range(UB):
                        for c in range(2):
                            last = mm(W0[:, b * P:(b + 1) * P], g[:, c, b * P:(b + 1) * P], wout[:, c, :],
                                      start=(c == 0), stop=(c == 1))
                    last.then_inc(S["mixed"], 1)
                if att:
                    score(UB * a + 3, 3)
                if mix:
                    pe.wait_ge(S["x1T_copied"], m + 1)
                    if post:
                        pe.wait_ge(S["ln2_sum"], q + 1)
                    elif att:
                        pe.wait_ge(S["qbd_ready"], a + 1)
                    if which[0] == -1:
                        pe.wait_ge(S["router_mm"], 1)
                    mm(W2, wqkvo[:, 0, :], x1T[:, :], start=True, stop=True).then_inc(S["q_ready"], 1)
                if att:
                    context(2)
                if mix:
                    if att:
                        pe.wait_ge(S["v_copied"], a + 1)
                    km = k if par == 0 else k + 1
                    pe.wait_ge(ct_in_s[mp], (km + 1) * 16)
                    mm(W1, wqkvo[:, 1, :], ct_in[:, mp, :], start=True, stop=True).then_inc(S["k_ready"], 1)
                if att:
                    context(3)
                if post:
                    pe.wait_ge(S["x2_ready"], q + 1)
                    if gate:
                        pe.wait_ge(S["ln1_var"], z + 1)
                    elif route:
                        pe.wait_ge(S["diff_ready"], r + 1)
                    for t in range(UB):
                        last = tr(W0[:, t * P:(t + 1) * P], x2[:, mp, t, 0:P], ident)
                    last.then_inc(S["x2T_ready"], 1)
                    pe.wait_ge(S["x2T_copied"], q + 1)
                    for t in range(UB):
                        last = mm(W0[:, t * NE:(t + 1) * NE], x2T[:, t, :], wr[:, :], start=True, stop=True)
                    last.then_inc(S["logits"], 1)
                if mix:
                    score(UB * a + UB, UB)

            schedule(pe, unit)

            pe.wait_ge(S["idx_ready"], UN)
            mm(W0[:, 0:NE], ones_b[:, :], seen[:, 1, :], start=True, stop=True).then_inc(S["counts"], 1)

            XT, Y = ps[:, 0, 0:P], ps[:, 7, 0:P]
            pe.wait_ge(S["table_ready"], 1)
            pe.wait_ge(S["experts_in"], 32)
            pe.wait_ge(S["bias_back"], 32)

            def turn_rows(t, k, slot):
                pe.wait_ge(rows_in[slot], 16 * (k + 1))
                at_least(pe, S["rowT_copied"], t)
                tr(XT, xr[:, slot, 0:P], ident).then_inc(S["rowT"], 1)

            turn_rows(0, 0, 0)

            def group(n, k, par):
                whole = isinstance(n, int)
                for s in range(GT):
                    t = n * GT + s
                    if not whole or t < NT:
                        e = pe.value_load(tab[0:1, 1, bass.ds(t, 1)], min_val=0, max_val=NE - 1)
                        if not whole or t >= GT:
                            at_least(pe, S["gelu"], t - GT + 1)
                        mm(ps[:, 1 + s, :], ones3[:, :], bias[:, bass.ds(e * FF, FF)], start=True, stop=False)
                        pe.wait_ge(S["rowT_copied"], t + 1)
                        mm(ps[:, 1 + s, :], xrT[:, s, :], w1s[:, bass.ds(e * FF, FF)],
                           start=False, stop=True).then_inc(S["hidden"], 1)
                    if not whole or (1 <= t < NT + 1):
                        sb_ = (s - 1) % GT
                        pe.wait_ge(S["gelu"], t)
                        if not whole or t - 1 >= GT:
                            at_least(pe, S["hidT_copied"], t - GT)
                        for c in range(FC):
                            last = tr(ps[:, 4 + sb_, c * P:(c + 1) * P], hg[:, sb_, c * P:(c + 1) * P], ident)
                        last.then_inc(S["hidT"], 1)
                    if not whole or (2 <= t < NT + 2):
                        sc = (s - 2) % GT
                        e = pe.value_load(tab[0:1, 1, bass.ds(t - 2, 1)], min_val=0, max_val=NE - 1)
                        if not whole or t > 2:
                            at_least(pe, S["res_ready"], t - 2)
                        mm(Y, ones3[:, :], bias[:, bass.ds(e * P + NE * FF, P)], start=True, stop=False)
                        pe.wait_ge(S["hidT_copied"], t - 1)
                        for c in range(FC):
                            last = mm(Y, hT[:, sc, c * P:(c + 1) * P], w2s[:, bass.ds(e * FF + c * P, P)],
                                      start=False, stop=(c == FC - 1))
                        last.then_inc(S["y_ready"], 1)
                    if not whole or t + 1 < NT:
                        if s < 2:
                            turn_rows(t + 1, k, par * GT + s + 1)
                        else:
                            turn_rows(t + 1, k if par == 0 else k + 1, (1 - par) * GT)

            schedule2(pe, group)

        @block.scalar
        def _(act):
            A = nc.scalar.activation
            link = Chain(act, S["act"])
            act.wait_ge(S["consts_in"], 80)
            link(A(dn[:, 0, :], alog[:, :, :].rearrange("p c n -> p (c n)"), ACT.Exp))
            act.wait_ge(S["delta_pre"], 1)
            A(v[:, 3, :], v[:, 2, :], ACT.Exp).then_inc(S["exp_a"], 1)
            act.wait_ge(S["exp_b"], 1)
            A(v[:, 5, :], v[:, 4, :], ACT.Ln).then_inc(S["ln_c"], 1)
            act.wait_ge(S["dax"], 1)
            A(dn[:, 3, :], dn[:, 2, :], ACT.Exp).then_inc(S["exp_a"], 1)

            def unit(a, k, par, which):
                z, m, q, r = a + 2, a + 1, a - 1, a - 2
                gate, mix, att, post, route = (runs(which, x) for x in (2, 1, 0, -1, -2))
                mp = 1 - par

                def exps(j):
                    i = UB * a + j
                    act.wait_ge(S["shifted"], i + 1)
                    A(E[:, j, :, :], E[:, j, :, :], ACT.Exp).then_inc(S["exp_ready"], 1)

                def heads(h0, h1):
                    for h in range(h0, h1):
                        last = A(qbd[:, mp, h, :, :], W2, ACT.Identity, scale=hmask[:, h:h + 1])
                    return last

                if route:
                    act.wait_ge(S["diff_ready"], r + 1)
                    A(er[:, :, :], df[:, :, :], ACT.Exp).then_inc(S["gate_exp"], 1)
                if mix:
                    act.wait_ge(S["ln1_shift"], m + 1)
                    at_least(act, S["x1T_ready"], m)
                    at_least(act, S["x1_kept"], m)
                    for b in range(UB):
                        last = A(x1[:, b, :], xs[:, b, :], ACT.Identity, bias=nb[:, b:b + 1], scale=rs[:, b:b + 1])
                    last.then_inc(S["x1_ready"], 1)
                if gate:
                    act.wait_ge(S["z_ready"], z + 1)
                    at_least(act, S["g_ready"], z)
                    A(th[:, :, :], ps[:, 4:6, :], ACT.Tanh, scale=0.5).then_inc(S["tanh_ready"], 1)
                if att:
                    exps(0)
                if mix:
                    act.wait_ge(S["x1T_ready"], m + 1)
                    at_least(act, S["q_ready"], m)
                    A(x1T[:, :], W1, ACT.Identity).then_inc(S["x1T_copied"], 1)
                if post:
                    act.wait_ge(S["ctx_ready"], UB * a)
                    at_least(act, S["proj"], q)
                    A(ctT[:, :, :], CT, ACT.Identity).then_inc(S["ctx_copied"], 1)
                if att:
                    exps(1)
                if att:
                    act.wait_ge(S["v_ready"], a + 1)
                    at_least(act, S["ctx_ready"], UB * (a - 1))
                    A(vbd[:, par, :, :].rearrange("p b (h w) -> p b h w", w=P + DH)[:, :, :, 0:DH],
                      W1, ACT.Identity).then_inc(S["v_copied"], 1)
                if mix:
                    act.wait_ge(S["x1_ready"], m + 1)
                    if post:
                        act.wait_ge(S["ln2_sum"], q + 1)
                    A(x1r[:, mp, :, :], x1[:, :, :], ACT.Identity).then_inc(S["x1_kept"], 1)
                    act.wait_ge(S["q_ready"], m + 1)
                    at_least(act, S["scores"], UB * (m - 1) if not isinstance(m, int) or m > 1 else 0)
                    heads(0, 4)
                if att:
                    exps(2)
                if mix:
                    act.wait_ge(S["k_ready"], m + 1)
                    at_least(act, S["scores"], UB * m)
                    A(kt[:, :, :], W1, ACT.Identity).then_inc(S["k_copied"], 1)
                if post:
                    act.wait_ge(S["ln2_shift"], q + 1)
                    if not isinstance(q, int) or q >= 2:
                        for t in range(UB):
                            act.wait_ge(rows_out[mp * UB + t], 16 * k)
                    for b in range(UB):
                        last = A(x2[:, mp, b, 0:P], xs2[:, b, :], ACT.Identity, bias=nb2[:, b:b + 1],
                                 scale=rs2[:, b:b + 1])
                    last.then_inc(S["x2_ready"], 1)
                if mix:
                    heads(4, H).then_inc(S["qbd_ready"], 1)
                if post:
                    act.wait_ge(S["x2T_ready"], q + 1)
                    at_least(act, S["logits"], q)
                    A(x2T[:, :, :], W0, ACT.Identity).then_inc(S["x2T_copied"], 1)
                if att:
                    exps(3)

            schedule(act, unit)

            def group(n, k, par):
                whole = isinstance(n, int)
                if not whole or 2 <= n:
                    act.wait_ge(S["shift3"], n - 1)
                    for s in range(GT):
                        slot = par * GT + s
                        if not whole or n >= 4:
                            act.wait_ge(final_out[slot], 16 * (k - 1))
                        A(ot[:, slot, :], rsd[:, slot, :], ACT.Identity, bias=nb3[:, slot:slot + 1],
                          scale=rs3[:, slot:slot + 1]).then_inc(S["out_ready"], 1)
                for s in range(GT):
                    t = n * GT + s
                    if whole and t >= NT:
                        continue
                    act.wait_ge(S["rowT"], t + 1)
                    if not whole or t >= GT:
                        at_least(act, S["hidden"], t - GT + 1)
                    A(xrT[:, s, :], ps[:, 0, 0:P], ACT.Identity).then_inc(S["rowT_copied"], 1)
                    act.wait_ge(S["hidden"], t + 1)
                    if not whole or t >= GT:
                        at_least(act, S["hidT"], t - GT + 1)
                    A(hg[:, s, :], ps[:, 1 + s, :], ACT.Gelu).then_inc(S["gelu"], 1)

            schedule2(act, group)

        @block.vector
        def _(dve):
            V = nc.vector
            link = Chain(dve, S["dve"])
            V.memset(ones_f[:, :], 1.0).then_inc(S["ones_done"], 1)
            V.memset(ones_b[:, :], 1.0)
            V.memset(mh[:, :], -0.5)
            V.memset(g8[:, 19:20], 0.5)
            link(V.memset(seen[:, :, :], 0.0))
            V.memset(dn[:, 7, :], 0.0)
            V.memset(pad[:, 0:P + 1], 0.0)
            link(V.memset(pad[:, P + 1:ROW], float(2 * TOK)))
            V.tensor_copy(pad[:, P:P + 1], pad[:, 0:1]).then_inc(S["pad_ready"], 1)
            dve.wait_ge(S["consts_in"], 80)
            V.tensor_copy(x2[:, 0, :, P + 1], ids)
            V.tensor_scalar(x2[:, 1, :, P + 1], ids, float(UT), None, ALU.add)
            link(V.tensor_copy(before[:, :], before_f))
            dve.wait_ge(S["mix_rows"], 1)
            V.tensor_copy(dbc[:, :], W0[:, 0:96])
            V.tensor_copy(dlt[:, :], W1[0:RANK, 0:1]).then_inc(S["mix_rows_copied"], 1)
            dve.wait_ge(S["delta_raw"], 1)
            link(V.tensor_tensor(v[:, 0, :], W2[:, 0:2], sm[:, 0:2], ALU.add))
            link(V.tensor_scalar(v[:, 1, :], v[:, 0, :], -1.0, None, ALU.mult))
            V.tensor_tensor(v[:, 2, :], v[:, 0, :], v[:, 1, :], ALU.min).then_inc(S["delta_pre"], 1)
            dve.wait_ge(S["exp_a"], 1)
            V.tensor_scalar(v[:, 4, :], v[:, 3, :], 1.0, None, ALU.add).then_inc(S["exp_b"], 1)
            dve.wait_ge(S["ln_c"], 1)
            dve.wait_ge(S["exp_b"], 1)
            link(V.tensor_scalar(v[:, 6, :], v[:, 4, :], -1.0, None, ALU.add))
            V.tensor_scalar(v[:, 7, :], v[:, 6, :], 0.0, None, ALU.is_le)
            link(V.tensor_scalar(v[:, 8, :], v[:, 6, :], 1e-30, None, ALU.max))
            link(V.reciprocal(v[:, 9, :], v[:, 8, :]))
            link(V.tensor_tensor(v[:, 10, :], v[:, 9, :], v[:, 5, :], ALU.mult))
            link(V.tensor_tensor(v[:, 11, :], v[:, 10, :], v[:, 7, :], ALU.add))
            link(V.tensor_tensor(v[:, 12, :], v[:, 11, :], v[:, 3, :], ALU.mult))
            link(V.scalar_tensor_tensor(v[:, 13, :], v[:, 0, :], 0.0, v[:, 12, :], ALU.max, ALU.add))
            delta = v[:, 13, :].unsqueeze(2).to_broadcast([P, 2, NST])
            dve.wait_ge(S["act"], 1)
            dn3 = dn[:, :, :].rearrange("p k (c n) -> p k c n", c=2)
            link(V.tensor_tensor(dn3[:, 1], dn3[:, 0], delta, ALU.mult))
            V.tensor_scalar(dn[:, 2, :], dn[:, 1, :], -1.0, None, ALU.mult).then_inc(S["dax"], 1)
            link(V.tensor_tensor(dn[:, 4, 0:NST], dbc[:, RANK:RANK + NST], dbc[:, RANK + NST:96], ALU.mult))
            pw3 = pw[:, :, :].rearrange("p (c n) t -> p c n t", c=2)
            link(V.tensor_tensor(pw3[:, :, :, 0], dn[:, 4, 0:NST].unsqueeze(1).to_broadcast([P, 2, NST]), delta, ALU.mult))
            dve.wait_ge(S["exp_a"], 2)
            w, src = 1, 3
            while w < P:
                link(V.tensor_tensor(pw[:, :, w:2 * w], pw[:, :, 0:w],
                                     dn[:, src, :].unsqueeze(2).to_broadcast([P, 2 * NST, w]), ALU.mult))
                nxt = 8 - src if src != 3 else 5
                nxt = {3: 5, 5: 6, 6: 5}[src]
                if 2 * w < P:
                    link(V.tensor_tensor(dn[:, nxt, :], dn[:, src, :], dn[:, src, :], ALU.mult))
                w, src = 2 * w, nxt
            link(V.tensor_reduce(wsum[:, :, :], pw3.rearrange("p c n t -> p c t n"), AX.X, ALU.add))
            for c in range(2):
                last = V.tensor_tensor_scan(yd[:, c, :], wsum[:, c, :], pw[:, 0, :], 0.0, ALU.add, ALU.bypass)
            link(last)
            for c in range(2):
                last = V.tensor_scalar(yd[:, c, :], yd[:, c, :], sm[:, 2 + c:3 + c], 0.5, ALU.add, ALU.mult)
            last.then_inc(S["yd_ready"], 1)
            dve.wait_ge(S["weights_in"], 80)
            link(V.tensor_tensor(g8[:, 0:16], wgs[:, :], wgs[:, :], ALU.mult))
            V.tensor_reduce(g8[:, 16:17], g8[:, 0:16], AX.X, ALU.add).then_inc(S["router_norm"], 1)
            dve.wait_ge(S["router_pow"], 1)
            link(V.tensor_scalar(g8[:, 18:19], g8[:, 17:18], 1e-4, None, ALU.max))
            link(V.reciprocal(g8[:, 18:19], g8[:, 18:19]))
            V.tensor_scalar(g8[:, 0:16], wgs[:, :], g8[:, 18:19], None, ALU.mult).then_inc(S["router_norm"], 1)
            dve.wait_ge(S["wg_turned"], 1)
            V.tensor_copy(wgT[:, :], CT[0:16, 0:NE]).then_inc(S["wgT_ready"], 1)
            dve.wait_ge(S["router_mm"], 1)
            link(V.tensor_copy(wr[:, :], CT[:, 16:16 + NE]))
            dve.wait_ge(S["bias_in"], 16)
            for n in range(3):
                link(V.tensor_copy(bp[:, n, :], bf[:, n, :]))
                if n < 2:
                    link(V.tensor_tensor(bf[:, n + 1, :], bf[:, n, :], bp[:, n, :], ALU.subtract))
            V.tensor_copy(pr[:, 0, :], wr[:, :]).then_inc(S["bias_out"], 1)

            def variance(st, mv, ve, done):
                V.tensor_tensor(mv[:, 0], st[:, :, 1], st[:, :, 4], ALU.add)
                V.tensor_tensor(mv[:, 1], st[:, :, 1], st[:, :, 4], ALU.subtract)
                link(V.tensor_tensor(mv[:, 2], st[:, :, 2], st[:, :, 5], ALU.add))
                link(V.tensor_tensor(mv[:, 3], mv[:, 1], mv[:, 1], ALU.mult))
                link(V.scalar_tensor_tensor(mv[:, 4], mv[:, 2], 4.0 / P, mv[:, 3], ALU.mult, ALU.add))
                V.tensor_scalar(ve, mv[:, 4], 0.25, EPS, ALU.mult, ALU.add).then_inc(done, 1)

            def layer_norm(xs, st, mv, ve, done):
                for b in range(UB):
                    last = V.bn_stats(st[:, b, :], xs[:, b, :])
                link(last)
                variance(st, mv, ve[:, :], done)

            def unit(a, k, par, which):
                z, m, q, r = a + 2, a + 1, a - 1, a - 2
                gate, mix, att, post, route = (runs(which, x) for x in (2, 1, 0, -1, -2))
                mp = 1 - par
                lg = W0[:, 0:UB * NE].rearrange("p (t e) -> p t e", t=UB)
                pos = W2[:, UB * NE:2 * UB * NE].rearrange("p (t e) -> p t e", t=UB)

                def shift(j):
                    i = UB * a + j
                    dve.wait_ge(S["scores"], i + 1)
                    pp = 2 * (j % 2)
                    link(V.tensor_reduce(mx[:, :], ps[:, pp:pp + 2, :].rearrange("p g (h q) -> p q (g h)", h=4),
                                         AX.X, ALU.max))
                    at_least(dve, S["ctx_ready"], i - 3)
                    V.tensor_tensor(E[:, j, :, :], ps[:, pp:pp + 2, :].rearrange("p g (h q) -> p (g h) q", h=4),
                                    mx[:, :].unsqueeze(1).to_broadcast([P, H, P]),
                                    ALU.subtract).then_inc(S["shifted"], 1)

                def inverse(j):
                    i = UB * a + j
                    jj, pp = (j - 1) % UB, (j - 1) % 2
                    dve.wait_ge(S["exp_ready"], i)
                    at_least(dve, S["attn_ready"], i - 2)
                    link(V.tensor_reduce(se[:, pp, :], E[:, jj, :, :].rearrange("p h q -> p q h"), AX.X, ALU.add))
                    V.reciprocal(re[:, pp, :], se[:, pp, :]).then_inc(S["recip_ready"], 1)

                if post:
                    inverse(0)
                if att:
                    shift(0)
                if route:
                    at_least(dve, S["onehot"], r + 1)
                    V.tensor_tensor(seen[:, par, :], seen[:, mp, :], cu[:, :], ALU.add)
                    dve.wait_ge(S["pos_ready"], r + 1)
                    link(V.tensor_tensor(pr[:, :, :], pos, oh[:, :, :], ALU.mult))
                    link(V.tensor_reduce(r4[:, 2, :], pr[:, :, :], AX.X, ALU.add))
                    link(V.scalar_tensor_tensor(r4[:, 3, :], r4[:, 1, :], float(-CAP), r4[:, 2, :],
                                                ALU.mult, ALU.add))
                    dve.wait_ge(S["gate_exp"], r + 1)
                    link(V.tensor_reduce(r4[:, 4, :], er[:, :, :], AX.X, ALU.add))
                    V.reciprocal(x2[:, par, :, P], r4[:, 4, :])
                    link(V.tensor_scalar(x2[:, par, :, P + 1], x2[:, par, :, P + 1], float(2 * UT), None, ALU.add))
                    V.tensor_scalar(idx[:, par, :], r4[:, 3, :], float(NE * CAP), None,
                                    ALU.add).then_inc(S["idx_ready"], 1)
                if gate:
                    dve.wait_ge(S["tanh_ready"], z + 1)
                    V.scalar_tensor_tensor(th[:, :, :], th[:, :, :], 1.0, ps[:, 4:6, :], ALU.add,
                                           ALU.mult).then_inc(S["u_ready"], 1)
                if att:
                    inverse(1)
                    shift(1)
                if post:
                    dve.wait_ge(S["proj"], q + 1)
                    at_least(dve, S["x2_ready"], q)
                    dve.wait_ge(S["x1_kept"], q + 1)
                    V.tensor_tensor(xs2[:, :, :], W2.rearrange("p (b d) -> p b d", b=UB),
                                    x1r[:, mp, :, :], ALU.add).then_inc(S["ln2_sum"], 1)
                    dve.wait_ge(S["ln2_sum"], q + 1)
                    layer_norm(xs2, st2, mv2, ve2, S["ln2_var"])
                if att:
                    inverse(2)
                    shift(2)
                if gate:
                    dve.wait_ge(S["mixed"], z + 1)
                    dve.wait_ge(xk_in[par], 16 * (k + 2))
                    at_least(dve, S["x1_ready"], z)
                    link(V.tensor_tensor(xs[:, :, :], W0.rearrange("p (b d) -> p b d", b=UB),
                                         xk[:, par, :].rearrange("p (b d) -> p b d", b=UB), ALU.add))
                    layer_norm(xs, st, mv, ve, S["ln1_var"])
                if post:
                    dve.wait_ge(S["ln2_rstd"], q + 1)
                    V.scalar_tensor_tensor(nb2[:, :], mv2[:, 0], -0.5, rs2[:, :], ALU.mult,
                                           ALU.mult).then_inc(S["ln2_shift"], 1)
                if att:
                    inverse(3)
                    shift(3)
                if gate:
                    dve.wait_ge(S["ln1_rstd"], z + 1)
                    V.scalar_tensor_tensor(nb[:, :], mv[:, 0], -0.5, rs[:, :], ALU.mult,
                                           ALU.mult).then_inc(S["ln1_shift"], 1)
                if post:
                    dve.wait_ge(S["logits"], q + 1)
                    link(V.tensor_reduce(r4[:, 0, :], lg, AX.X, ALU.max))
                    V.tensor_tensor(df[:, :, :], lg, r4[:, 0, :].unsqueeze(2).to_broadcast([P, UB, NE]),
                                    ALU.subtract).then_inc(S["diff_ready"], 1)
                    dve.wait_ge(S["diff_ready"], q + 1)
                    link(V.scalar_tensor_tensor(rk[:, :, :].rearrange("p t e -> p (t e)"),
                                                df[:, :, :].rearrange("p t e -> p (t e)"), 0.0, rank,
                                                ALU.is_ge, ALU.mult))
                    link(V.tensor_reduce(r4[:, 1, :], rk[:, :, :], AX.X, ALU.max))
                    link(V.tensor_tensor(oh[:, :, :], rank.rearrange("p (t e) -> p t e", t=UB),
                                         r4[:, 1, :].unsqueeze(2).to_broadcast([P, UB, NE]), ALU.is_equal))
                    V.tensor_reduce(cu[:, :], oh[:, :, :].rearrange("p t e -> p e t"), AX.X,
                                    ALU.add).then_inc(S["onehot"], 1)

            schedule(dve, unit, link, VECTOR_STEPS)

            dve.wait_ge(S["counts"], 1)
            link(V.tensor_copy(cn[:, 0, :], W0[:, 0:NE]))
            link(V.tensor_scalar(cn[:, 1, :], rank[:, 0:NE], float(-CAP),
                                 float(NE * CAP), ALU.mult, ALU.add))
            link(V.tensor_tensor(cn[:, 2, :], cn[:, 1, :], cn[:, 0, :], ALU.add))
            V.tensor_scalar(pidx[:, :], cn[:, 2, :], ids[:, 0:1],
                            float(2 * UT), ALU.add, ALU.add).then_inc(S["counts"], 1)
            link(V.tensor_scalar(cn[0:1, 3, :], cn[0:1, 0, :], float(P - 1), 1.0 / P, ALU.add, ALU.mult))
            link(V.tensor_scalar(cni[:, :], cn[0:1, 3, :], 1.0 / 256 - 0.5, None, ALU.add))
            link(V.tensor_copy(cn[0:1, 4, :], cni[:, :]))
            link(V.tensor_tensor_scan(cn[0:1, 5, :], cn[0:1, 4, :], cn[0:1, 4, :], 0.0, ALU.add, ALU.bypass))
            g3 = ge[:, :, :].rearrange("p k (t e) -> p k t e", e=NE)
            link(V.tensor_tensor(g3[:, 0], tnum.rearrange("p (t e) -> p t e", e=NE),
                                 cn[0:1, 5, :].unsqueeze(1).to_broadcast([1, NT, NE]), ALU.is_ge))
            link(V.tensor_reduce(tb[:, 0, :], g3[:, 0], AX.X, ALU.add))
            link(V.tensor_tensor(g3[:, 1], g3[:, 0],
                                 cn[0:1, 4, :].unsqueeze(1).to_broadcast([1, NT, NE]), ALU.mult))
            link(V.tensor_reduce(tb[:, 1, :], g3[:, 1], AX.X, ALU.add))
            link(V.tensor_tensor(tb[:, 2, :], tnum.rearrange("p (t e) -> p t e", e=NE)[:, :, 0], tb[:, 1, :], ALU.subtract))
            link(V.tensor_scalar(tb[:, 3, :], tb[:, 0, :], float(CAP), None, ALU.mult))
            link(V.scalar_tensor_tensor(tb[:, 4, :], tb[:, 2, :], float(P), tb[:, 3, :], ALU.mult, ALU.add))
            link(V.tensor_scalar(tab[:, 0, :], tb[:, 4, :], float(NE * CAP), None, ALU.min))
            V.tensor_scalar(tab[:, 1, :], tb[:, 0, :], float(NE - 1), None, ALU.min).then_inc(S["table_ready"], 1)

            def group(n, k, par):
                whole = isinstance(n, int)
                for s in range(GT):
                    t = n * GT + s
                    if s == 0 and (not whole or n >= 2):
                        dve.wait_ge(S["rstd3"], n - 1)
                        lo, hi = par * GT, par * GT + GT
                        V.scalar_tensor_tensor(nb3[:, lo:hi], mv3[:, 0, lo:hi], -0.5, rs3[:, lo:hi],
                                               ALU.mult, ALU.mult).then_inc(S["shift3"], 1)
                    if not whole or 1 <= t < NT + 1:
                        sb_ = (s - 1) % GT
                        dve.wait_ge(S["hidT"], t)
                        if not whole or t - 1 >= GT:
                            at_least(dve, S["y_ready"], t - GT)
                        V.tensor_copy(hT[:, sb_, :], ps[:, 4 + sb_, :]).then_inc(S["hidT_copied"], 1)
                    if not whole or 2 <= t < NT + 2:
                        slot = (par * GT + s - 2) % NX
                        kk = k if s == 2 or par == 1 else k - 1
                        dve.wait_ge(S["y_ready"], t - 1)
                        if not whole or t - 2 >= NX:
                            at_least(dve, S["out_ready"], t - 2 - NX + 1)
                            dve.wait_ge(final_out[slot], 16 * kk)
                        link(V.tensor_copy(tix[:, slot:slot + 1], xr[:, slot, P + 1:ROW]))
                        V.scalar_tensor_tensor(rsd[:, slot, :], ps[:, 7, 0:P], xr[:, slot, P:P + 1],
                                               xr[:, slot, 0:P], ALU.mult, ALU.add).then_inc(S["res_ready"], 1)
                        dve.wait_ge(S["res_ready"], t - 1)
                        link(V.bn_stats(st3[:, slot, :], rsd[:, slot, :]))
                    if s == 1 and (not whole or 1 <= n <= NG):
                        lo = (1 - par) * GT
                        variance(st3[:, lo:lo + GT, :], mv3[:, :, lo:lo + GT], ve3[:, lo:lo + GT], S["var3"])

            schedule2(dve, group, link, VECTOR_STEPS_2)

        @block.gpsimd
        def _(pool):
            G = nc.gpsimd
            G.memset(vbd[:, 0, :, :], 0.0)
            G.memset(vbd[:, 1, :, :], 0.0)
            G.memset(bias[:, :], 0.0)
            G.memset(ones3[:, :], 0.0).then_inc(S["memset_done"], 1)
            pool.wait_ge(S["memset_done"], 1)
            G.memset(ones3[0:3, :], 1.0).then_inc(S["memset_done"], 1)
            G.iota(tailx[:, :], pattern=[[QR, UB]], base=NE * CAP, channel_multiplier=1).then_inc(S["memset_done"], 1)
            pool.wait_ge(S["pad_ready"], 1)
            pool.wait_ge(S["memset_done"], 3)
            for t in range(UB):
                G.indirect_dma_start(out=lists, out_offset=bass.IndirectOffsetOnAxis(ap=tailx[:, t:t + 1], axis=0),
                                     in_=pad[0:QR, :], in_offset=None).then_inc(rows_out[UB + t], 16)
            pool.wait_ge(S["router_norm"], 1)
            G.tensor_tensor(g8[:, 17:18], g8[:, 16:17], g8[:, 19:20], ALU.pow).then_inc(S["router_pow"], 1)

            def unit(a, k, par, which):
                z, m, q, r = a + 2, a + 1, a - 1, a - 2
                gate, mix, att, post, route = (runs(which, x) for x in (2, 1, 0, -1, -2))
                mp = 1 - par

                def normalize(j):
                    i = UB * a + j
                    jj, pp = (j - 1) % UB, (j - 1) % 2
                    pool.wait_ge(S["recip_ready"], i)
                    G.tensor_tensor(E[:, jj, :, :], E[:, jj, :, :],
                                    re[:, pp, :].unsqueeze(1).to_broadcast([P, H, P]),
                                    ALU.mult).then_inc(S["attn_ready"], 1)

                def scatter(first, count):
                    if route:
                        for t in range(first, first + count):
                            G.indirect_dma_start(
                                out=lists, out_offset=bass.IndirectOffsetOnAxis(ap=idx[:, par, t:t + 1], axis=0),
                                in_=x2[:, par, t, :], in_offset=None).then_inc(rows_out[par * UB + t], 16)

                if post:
                    normalize(0)
                if gate:
                    pool.wait_ge(S["u_ready"], z + 1)
                    at_least(pool, S["mixed"], z)
                    if which[0] == -2:
                        pool.wait_ge(S["yd_ready"], 1)
                    for c in range(2):
                        last = G.tensor_tensor(g[:, c, :].rearrange("p (b l) -> p b l", b=UB),
                                               th[:, c, :].rearrange("p (b l) -> p b l", b=UB),
                                               yd[:, c, :].unsqueeze(1).to_broadcast([P, UB, P]), ALU.mult)
                    last.then_inc(S["g_ready"], 1)
                if att:
                    normalize(1)
                if post:
                    pool.wait_ge(S["ln2_var"], q + 1)
                    at_least(pool, S["x2_ready"], q)
                    if route:
                        pool.wait_ge(S["idx_ready"], r + 1)
                    G.tensor_tensor(rs2[:, :], ve2[:, :], mh[:, :], ALU.pow).then_inc(S["ln2_rstd"], 1)
                if att:
                    normalize(2)
                if route and not post:
                    pool.wait_ge(S["idx_ready"], r + 1)
                scatter(0, 2)
                if gate:
                    pool.wait_ge(S["ln1_var"], z + 1)
                    at_least(pool, S["x1_ready"], z)
                    G.tensor_tensor(rs[:, :], ve[:, :], mh[:, :], ALU.pow).then_inc(S["ln1_rstd"], 1)
                if att:
                    normalize(3)
                scatter(2, 2)

            schedule(pool, unit)

            pool.wait_ge(S["counts"], 2)
            for e in range(NE):
                G.indirect_dma_start(out=lists, out_offset=bass.IndirectOffsetOnAxis(ap=pidx[:, e:e + 1], axis=0),
                                     in_=pad[:, :], in_offset=None).then_inc(S["pads_out"], 16)

            def group(n, k, par):
                whole = isinstance(n, int)
                if not whole or 1 <= n <= NG:
                    lo = (1 - par) * GT
                    pool.wait_ge(S["var3"], n)
                    if not whole or 2 <= n:
                        pool.wait_ge(S["out_ready"], (n - 1) * GT)
                    G.tensor_tensor(rs3[:, lo:lo + GT], ve3[:, lo:lo + GT], mh[:, 0:GT],
                                    ALU.pow).then_inc(S["rstd3"], 1)
                if not whole or 2 <= n:
                    if whole and n > NG:
                        pool.wait_ge(S["out_ready"], (n - 1) * GT)
                    for s in range(GT):
                        slot = par * GT + s
                        G.indirect_dma_start(
                            out=out, out_offset=bass.IndirectOffsetOnAxis(ap=tix[:, slot:slot + 1], axis=0),
                            in_=ot[:, slot, :], in_offset=None, bounds_check=TOK - 1,
                            oob_is_err=False).then_inc(final_out[slot], 16)

            schedule2(pool, group)
            for slot in range(NX):
                pool.wait_ge(final_out[slot], 16 * ((NG + (slot < GT)) // 2))
            for n, q in enumerate(rows_out):
                pool.wait_ge(q, 16 * (UN // 2 + n // UB))
            pool.wait_ge(S["pads_out"], 16 * NE)
            pool.wait_ge(S["bias_back"], 32)


VECTOR_STEPS = 52
VECTOR_STEPS_2 = 18


def constants():
    f = np.float32
    p = np.arange(P)
    hmask = (p[:, None] // DH == np.arange(H)[None, :]).astype(f) * f(DH ** -0.5)
    rank = np.tile(NE - np.arange(NE), UB)[None, :].repeat(P, 0).astype(f)
    ids = (p[:, None] + P * np.arange(UB)[None, :] - 2 * UT).astype(f)
    tnum = np.repeat(np.arange(NT), NE)[None, :].repeat(P, 0).astype(f)
    before = (p[:, None] < p[None, :]).astype(f)
    rest = np.zeros((P, 4), f)
    rest[:, 0], rest[:, 1] = 1.0, -0.5
    return np.ascontiguousarray(np.concatenate(
        [np.eye(P, dtype=f), before, hmask, rank, ids, tnum, rest], 1))


def kernel(x, ctx_1024, L0_attn_W_in, L0_attn_conv_w, L0_attn_conv_b, L0_attn_W_x, L0_attn_W_dt,
           L0_attn_b_dt, L0_attn_A_log, L0_attn_D_skip, L0_attn_W_out, L0_xattn_W_Q, L0_xattn_W_K,
           L0_xattn_W_V, L0_xattn_W_O, L0_ffn_w_red, L0_ffn_wg, L0_ffn_w1, L0_ffn_b1, L0_ffn_w2, L0_ffn_b2):
    import concourse.bacc as bacc
    from concourse.bass_utils import run_bass_kernel_spmd

    def c(a):
        return np.ascontiguousarray(a)

    x, ctx_1024 = np.asarray(x), np.asarray(ctx_1024)
    chunks = lambda a: c(np.asarray(a).reshape(2, P, -1).transpose(1, 0, 2))
    t = lambda a: np.asarray(a).T
    w1, w2 = np.asarray(L0_ffn_w1), np.asarray(L0_ffn_w2)
    ins = {
        "x_t": c(x.transpose(2, 0, 1).reshape(P, TOK)),
        "x_tok": c(x.transpose(1, 0, 2).reshape(P, TOK)),
        "ctx_t": c(ctx_1024.transpose(2, 0, 1).reshape(P, TOK)),
        "wz_t": c(t(L0_attn_W_in)[:, EI:]),
        "wx_t": chunks(t(L0_attn_W_x)),
        "wdt_t": c(t(L0_attn_W_dt)),
        "small": c(np.concatenate([np.asarray(L0_attn_b_dt).reshape(2, P).T,
                                   np.asarray(L0_attn_D_skip).reshape(2, P).T], 1)),
        "a_log": chunks(L0_attn_A_log),
        "wout_t": chunks(t(L0_attn_W_out)),
        "wqkvo_t": c(np.stack([t(L0_xattn_W_Q), t(L0_xattn_W_K), t(L0_xattn_W_V), t(L0_xattn_W_O)], 1)),
        "wred_t": c(t(L0_ffn_w_red)),
        "wg": c(np.asarray(L0_ffn_wg)),
        "w1": c(w1.transpose(1, 0, 2).reshape(P, NE * FF)),
        "w2": c(w2.reshape(NE, FC, P, P).transpose(2, 0, 1, 3).reshape(P, NE * FC * P)),
        "b12": c(np.concatenate([np.asarray(L0_ffn_b1).reshape(-1), np.asarray(L0_ffn_b2).reshape(-1)]).reshape(P, -1)),
        "consts": constants(),
    }
    nc = bacc.Bacc("TRN2", target_bir_lowering=False, num_devices=1)
    args = [nc.dram_tensor("in_" + n, a.shape, mybir.dt.from_np(a.dtype), kind="ExternalInput").ap()
            for n, a in ins.items()]
    out = nc.dram_tensor("out", [TOK, P], F32, kind="ExternalOutput").ap()
    decoder_program(nc, *args, out)
    r = run_bass_kernel_spmd(nc, [{"in_" + n: a for n, a in ins.items()}], core_ids=[0])
    return r.results[0]["out"].reshape(NSEQ, P, P)
```

```python
from contextlib import ExitStack

import numpy as np

import concourse.bass as bass
from concourse import mybir

ALU = mybir.AluOpType
ACT = mybir.ActivationFunctionType
AX = mybir.AxisListType
F32 = mybir.dt.float32
BF16 = mybir.dt.bfloat16
I32 = mybir.dt.int32
U32 = mybir.dt.uint32

P = 128
NSEQ = 32
UB = 4
UN = NSEQ // UB
UT = UB * P
H, DH = 8, 16
EI, NST, RANK = 256, 16, 64
NE, FF = 8, 512
FC = FF // P
TOK = NSEQ * P
CAP = TOK + P
ROW = P + 2
NT = TOK // P + NE - 1
GT = 3
NG = NT // GT
QR = P // UB
EPS = 1e-5


def at_least(eng, sem, n):
    if isinstance(n, int) and n <= 0:
        return
    eng.wait_ge(sem, n)


class Chain:

    def __init__(self, eng, sem):
        self.eng, self.sem, self.done, self.n = eng, sem, 0, 0

    def __call__(self, ins):
        self.n += 1
        ins.then_inc(self.sem, 1)
        self.eng.wait_ge(self.sem, self.done + self.n)

    def enter(self, rounds, per_round):
        self.before, self.per_round = self.done + self.n, per_round
        self.done, self.n = self.before + rounds * per_round, 0

    def leave(self, rounds):
        assert self.n == self.per_round, f"a round has {self.n} steps"
        self.done, self.n = self.before + rounds * self.per_round, 0


def decoder_program(nc, x_t, x_tok, ctx_t, wz_t, wx_t, wdt_t, small, a_log, wout_t, wqkvo_t,
                    wred_t, wg, w1, w2, b12, consts, out):
    ctx = ExitStack()
    with ctx:
        def sb(name, shape, dt=F32):
            return ctx.enter_context(nc.sbuf_tensor(name, shape, dt))

        def sem(name):
            return ctx.enter_context(nc.semaphore(name))

        lists = nc.dram_tensor("expert_lists", [(NE + 1) * CAP, ROW], F32, kind="Internal").ap()
        bias_parts = nc.dram_tensor("bias_parts", [3, NE * (FF + P)], BF16, kind="Internal").ap()

        ps = ctx.enter_context(nc.psum_tensor("ps", [P, 8, 512], F32))
        W0, W1, W2, CT = ps[:, 4, :], ps[:, 5, :], ps[:, 6, :], ps[:, 7, :]

        wz = sb("wz", [P, EI]); wx = sb("wx", [P, 2, 96]); wdt = sb("wdt", [RANK, EI])
        sm = sb("sm", [P, 4])
        alog = sb("alog", [P, 2, NST]); wout = sb("wout", [P, 2, P])
        wqkvo = sb("wqkvo", [P, 4, P]); wred = sb("wred", [16, P]); wgs = sb("wgs", [NE, 16])
        w1s = sb("w1s", [P, NE * FF]); w2s = sb("w2s", [P, NE * FC * P])
        CW = 2 * P + 8 + 32 + 4 + 39 * 8 + 4
        cst = sb("cst", [P, CW])
        o = 0
        ident = cst[:, o:o + P]; o += P
        before_f = cst[:, o:o + P]; o += P
        hmask = cst[:, o:o + H]; o += H
        rank = cst[:, o:o + UB * NE]; o += UB * NE
        ids = cst[:, o:o + UB]; o += UB
        tnum = cst[0:1, o:o + NT * NE]; o += NT * NE
        ones_c = cst[:, o:o + 1]; o += 4

        ones_b = sb("ones_b", [P, P], BF16); before = sb("before", [P, P], BF16)
        ones3 = sb("ones3", [P, P], BF16)
        ones_f = sb("ones_f", [P, P])
        mh = sb("mh", [P, 4])

        dbc = sb("dbc", [P, 96]); dlt = sb("dlt", [RANK, 1])
        v = sb("v", [P, 14, 2]); dn = sb("dn", [P, 8, 2 * NST])
        yd = sb("yd", [P, 2, P]); wsum = sb("wsum", [P, 2, P])
        wr = sb("wr", [P, NE]); g8 = sb("g8", [NE, 20]); wgT = sb("wgT", [16, NE])
        xt = sb("xt", [P, 2, UT]); xk = sb("xk", [P, 2, UT]); ct_in = sb("ct_in", [P, 2, UT])
        zs = sb("zs", [P, 2, UT]); sg = sb("sg", [P, 2, UT]); g = sb("g", [P, 2, UT])
        xs = sb("xs", [P, UB, P]); st = sb("st", [P, UB, 6]); mv = sb("mv", [P, 4, UB])
        ve = sb("ve", [P, UB]); rs = sb("rs", [P, UB]); nb = sb("nb", [P, UB])
        xs2 = sb("xs2", [P, UB, P]); st2 = sb("st2", [P, UB, 6]); mv2 = sb("mv2", [P, 4, UB])
        ve2 = sb("ve2", [P, UB]); rs2 = sb("rs2", [P, UB]); nb2 = sb("nb2", [P, UB])
        x1 = sb("x1", [P, UB, P]); x1r = sb("x1r", [P, 2, UB, P]); x1T = sb("x1T", [P, UT])
        qbd = sb("qbd", [P, 2, H, UB, P]); kt = sb("kt", [P, UB, P])
        VW = H * (P + DH)
        vbd = sb("vbd", [P, 2, UB, VW])
        mx = sb("mx", [P, P]); E = sb("E", [P, 4, H, P]); se = sb("se", [P, 2, P])
        pw = E[:, :, :, :].rearrange("p j h q -> p (j h) q")
        re = sb("re", [P, 2, P]); ctT = sb("ctT", [P, UB, P])
        x2 = sb("x2", [P, 2, UB, ROW]); x2T = sb("x2T", [P, UB, P])
        df = sb("df", [P, UB, NE]); er = sb("er", [P, UB, NE]); rk = sb("rk", [P, UB, NE])
        r4 = sb("r4", [P, 6, UB]); oh = sb("oh", [P, UB, NE], BF16)
        seen = sb("seen", [P, 2, NE], BF16); cu = sb("cu", [P, NE]); pr = sb("pr", [P, UB, NE])
        idx = sb("idx", [P, 2, UB], U32)
        pad = sb("pad", [P, ROW]); tailx = sb("tailx", [QR, UB], U32)
        tb = sb("tb", [1, 12, NT]); cn = sb("cn", [P, 8, NE]); cni = sb("cni", [1, NE], I32)
        ge = sb("ge", [1, 2, NT * NE]); tab = sb("tab", [1, 2, NT], I32); pad_at = sb("pad_at", [1, NE], I32)
        BW = NE * (FF + P) // P
        bf = sb("bf", [P, 3, BW]); bp = sb("bp", [P, 3, BW], BF16)
        bias = sb("bias", [P, NE * (FF + P)], BF16)
        NX = 2 * GT
        xr = sb("xr", [P, NX, ROW]); xrT = sb("xrT", [P, GT, P])
        q0 = qbd[:, 0, :, :, :].rearrange("p h b q -> p (h b q)")
        q1 = qbd[:, 1, :, :, :].rearrange("p h b q -> p (h b q)")
        hg = q0[:, 0:GT * FF].rearrange("p (s f) -> p s f", s=GT)
        hT = q0[:, GT * FF:2 * GT * FF].rearrange("p (s f) -> p s f", s=GT)
        rsd = q1[:, 0:NX * P].rearrange("p (s f) -> p s f", s=NX)
        ot = q1[:, NX * P:2 * NX * P].rearrange("p (s f) -> p s f", s=NX)
        tix = sb("tix", [P, NX], U32)
        tnew = sb("tnew", [P, NX], U32)
        st3 = sb("st3", [P, NX, 6]); mv3 = sb("mv3", [P, 4, NX])
        ve3 = sb("ve3", [P, NX]); rs3 = sb("rs3", [P, NX]); nb3 = sb("nb3", [P, NX])

        S = {n: sem(n) for n in (
            "consts_in weights_in experts_in bias_in bias_out bias_back memset_done ones_done mix_rows mix_rows_copied "
            "delta_pre delta_raw exp_a exp_b ln_c dax yd_ready router_norm router_pow wg_turned wgT_ready "
            "router_mm "
            "z_ready z_copied z_scaled gate_ready g_ready mixed ln1_var ln1_rstd ln1_shift x1_ready x1_kept x1T_ready "
            "x1T_copied q_ready qbd_ready k_ready k_copied v_ready v_copied "
            "scores shifted exp_ready recip_ready attn_ready ctx_ready ctx_copied "
            "proj ln2_sum ln2_var ln2_rstd ln2_shift x2_ready x2T_ready x2T_copied logits diff_ready "
            "gate_exp onehot pos_ready idx_ready pads_out pad_ready counts table_ready "
            "dve act pool rowT rowT_copied hidden gelu hidT hidT_copied y_ready res_ready var3 rstd3 "
            "shift3 out_ready").split()}
        xt_in = [sem(f"xt_in{p}") for p in range(2)]
        xk_in = [sem(f"xk_in{p}") for p in range(2)]
        ct_in_s = [sem(f"ctx_in{p}") for p in range(2)]
        rows_out = [sem(f"rows_out{k}") for k in range(2 * UB)]
        rows_in = [sem(f"rows_in{k}") for k in range(NX)]
        final_out = [sem(f"final_out{k}") for k in range(NX)]

        def schedule(eng, unit, chain=None, per_round=0):
            for a in (-2, -1, 0, 1):
                unit(a, a // 2, a % 2, range(a, a + 1))
            with eng.Fori(1, 3) as k:
                if chain:
                    chain.enter(k - 1, per_round)
                unit(2 * k, k, 0, range(2, 5))
                unit(2 * k + 1, k, 1, range(3, 6))
                if chain:
                    chain.leave(2)
            for a in (6, 7, 8, 9):
                unit(a, a // 2, a % 2, range(a, a + 1))

        def runs(which, shift):
            return 0 <= which[0] + shift < UN

        def schedule2(eng, group, chain=None, per_round=0):
            for n in range(5):
                group(n, n // 2, n % 2)
            with eng.Fori(2, NG // 2 - 1) as k:
                if chain:
                    chain.enter(k - 2, per_round)
                group(2 * k + 1, k, 1)
                group(2 * k + 2, k + 1, 0)
                if chain:
                    chain.leave(NG // 2 - 3)
            for n in range(NG - 2, NG + 2):
                group(n, n // 2, n % 2)

        block = ctx.enter_context(nc.Block())

        @block.sync
        def _(sp):
            def load(n, par):
                cols = bass.ds(n * UT, UT)
                at_least(sp, S["z_ready"], n - 1 if not isinstance(n, int) or n > 1 else 0)
                sp.dma_start(xt[:, par, :], x_t[:, cols]).then_inc(xt_in[par], 16)
                at_least(sp, S["ln1_var"], n - 1 if not isinstance(n, int) or n > 1 else 0)
                sp.dma_start(xk[:, par, :], x_tok[:, cols]).then_inc(xk_in[par], 16)
                at_least(sp, S["v_ready"], n - 1 if not isinstance(n, int) or n > 1 else 0)
                sp.dma_start(ct_in[:, par, :], ctx_t[:, cols]).then_inc(ct_in_s[par], 16)

            sp.dma_start(wx[:, :, :], wx_t).then_inc(S["consts_in"], 16)
            sp.dma_start(wdt[:, :], wdt_t).then_inc(S["consts_in"], 16)
            sp.dma_start(sm[:, :], small).then_inc(S["consts_in"], 16)
            sp.dma_start(alog[:, :, :], a_log).then_inc(S["consts_in"], 16)
            sp.dma_start(cst[:, :], consts).then_inc(S["consts_in"], 16)
            sp.dma_start(wz[:, :], wz_t).then_inc(S["weights_in"], 16)
            load(0, 0)
            sp.dma_start(wout[:, :, :], wout_t).then_inc(S["weights_in"], 16)
            sp.dma_start(wqkvo[:, :, :], wqkvo_t).then_inc(S["weights_in"], 16)
            sp.dma_start(wred[:, :], wred_t).then_inc(S["weights_in"], 16)
            sp.dma_start(wgs[:, :], wg).then_inc(S["weights_in"], 16)
            load(1, 1)
            sp.dma_start(bf[:, 0, :], b12).then_inc(S["bias_in"], 16)
            sp.dma_start(w1s[:, :], w1).then_inc(S["experts_in"], 16)
            sp.dma_start(w2s[:, :], w2).then_inc(S["experts_in"], 16)
            sp.wait_ge(S["bias_out"], 1)
            sp.dma_start(bias_parts.rearrange("k (p f) -> p k f", p=P), bp[:, :, :]).then_inc(S["bias_back"], 16)
            sp.wait_ge(S["bias_back"], 16)
            sp.wait_ge(S["memset_done"], 4)
            sp.dma_start(bias[0:3, :], bias_parts).then_inc(S["bias_back"], 16)
            with sp.Fori(1, UN // 2) as k:
                load(2 * k, 0)
                load(2 * k + 1, 1)

            sp.wait_ge(S["pad_ready"], 1)
            sp.wait_ge(S["counts"], 2)
            for e in range(NE // 2):
                at = sp.value_load(pad_at[0:1, e:e + 1], min_val=0, max_val=NE * CAP)
                sp.dma_start(lists[bass.ds(at, P), :], pad[:, :]).then_inc(S["pads_out"], 16)

            sp.wait_ge(S["table_ready"], 1)
            first = sp.value_load(tab[0:1, 0, 0:1], min_val=0, max_val=NE * CAP)
            for n, q in enumerate(rows_out):
                sp.wait_ge(q, 16 * (UN // 2 + n // UB))
            sp.wait_ge(S["pads_out"], 16 * NE)

            def group(n, k, par):
                if isinstance(n, int) and n >= NG:
                    return
                for s in range(GT):
                    t = n * GT + s
                    slot = par * GT + s
                    if not (isinstance(n, int) and n < 2):
                        at_least(sp, S["res_ready"], t - NX + 1)
                    if isinstance(t, int) and t == 0:
                        at = first
                    else:
                        at = sp.value_load(tab[0:1, 0, bass.ds(t, 1)], min_val=0, max_val=NE * CAP)
                    sp.dma_start(xr[:, slot, :], lists[bass.ds(at, P), :]).then_inc(rows_in[slot], 16)

            group(0, 0, 0)
            group(1, 0, 1)
            with sp.Fori(1, (NG + 1) // 2 - 1) as k:
                group(2 * k, k, 0)
                group(2 * k + 1, k, 1)
            group(NG - 1, NG // 2, 0)

        @block.tensor
        def _(pe):
            mm, tr = nc.tensor.matmul, nc.tensor.transpose
            pe.wait_ge(S["consts_in"], 80)
            pe.wait_ge(S["ones_done"], 1)
            for c in range(2):
                mm(W0[:, 0:96], ones_f[:, :], wx[:, c, :], start=(c == 0), stop=(c == 1))
            for c in range(2):
                last = mm(W1[0:RANK, 0:1], wx[:, c, 0:RANK], ones_f[:, 0:1], start=(c == 0), stop=(c == 1))
            last.then_inc(S["mix_rows"], 1)
            pe.wait_ge(S["mix_rows_copied"], 1)
            for c in range(2):
                last = mm(W2[:, c:c + 1], wdt[:, c * P:(c + 1) * P], dlt[:, :], start=True, stop=True)
            last.then_inc(S["delta_raw"], 1)

            def router():
                pe.wait_ge(S["router_norm"], 2)
                pe.wait_ge(S["weights_in"], 80)
                tr(CT[0:16, 0:NE], g8[:, 0:16], ident[0:NE, 0:NE]).then_inc(S["wg_turned"], 1)
                pe.wait_ge(S["wgT_ready"], 1)
                mm(CT[:, 16:16 + NE], wred[:, :], wgT[:, :], start=True, stop=True).then_inc(S["router_mm"], 1)

            def unit(a, k, par, which):
                z, m, q, r = a + 2, a + 1, a - 1, a - 2
                gate, mix, att, post, route = (runs(which, x) for x in (2, 1, 0, -1, -2))
                mp = 1 - par
                mixer_out = ps[:, 4 + which[0], :] if which[0] < 0 else W0

                def score(i, first):
                    jj = first % UB
                    pp = par if first < UB else mp
                    if first == UB:
                        pe.wait_ge(S["qbd_ready"], m + 1)
                        pe.wait_ge(S["k_copied"], m + 1)
                    at_least(pe, S["shifted"], i - 1)
                    for hh in range(2):
                        last = mm(ps[:, 2 * (jj % 2) + hh, :], kt[:, jj, :],
                                  qbd[:, pp, 4 * hh:4 * hh + 4, jj, :], start=True, stop=True)
                    last.then_inc(S["scores"], 1)

                def context(j):
                    jj, vp = (j - 2) % UB, par if j >= 2 else mp
                    pe.wait_ge(S["attn_ready"], UB * a + j - 1)
                    if j == 2:
                        pe.wait_ge(S["v_copied"], a + 1)
                        at_least(pe, S["ctx_copied"], a)
                    for h in range(H):
                        last = mm(CT[:, jj * P:(jj + 1) * P], vbd[:, vp, jj, h * P:(h + 1) * P],
                                  E[:, jj, h, :], start=(h == 0), stop=(h == H - 1))
                    last.then_inc(S["ctx_ready"], 1)

                if gate:
                    pe.wait_ge(xt_in[par], (k + 2) * 16)
                    if which[0] > 0:
                        at_least(pe, S["ln1_var"], z)
                    if route:
                        pe.wait_ge(S["x2T_copied"], r + 1)
                    if att:
                        pe.wait_ge(S["k_copied"], a + 1)
                    if which[0] == -2:
                        pe.wait_ge(S["weights_in"], 80)
                    mm(W0, wz[:, 0:P], xt[:, par, :], start=True, stop=True)
                    mm(W1, wz[:, P:2 * P], xt[:, par, :], start=True, stop=True).then_inc(S["z_ready"], 1)
                if which[0] == -2:
                    router()
                if post:
                    context(0)
                if att:
                    if which[0] == 0:
                        pe.wait_ge(S["ln1_var"], 2)
                    score(UB * a + 1, 1)
                if post:
                    context(1)
                if mix:
                    pe.wait_ge(S["x1_ready"], m + 1)
                    if gate:
                        pe.wait_ge(S["z_copied"], z + 1)
                    elif att:
                        pe.wait_ge(S["k_copied"], a + 1)
                    for b in range(UB):
                        last = tr(W1[:, b * P:(b + 1) * P], x1[:, b, :], ident)
                    last.then_inc(S["x1T_ready"], 1)
                if post:
                    pe.wait_ge(S["ctx_copied"], q + 1)
                    if route:
                        pe.wait_ge(S["diff_ready"], r + 1)
                    if att:
                        pe.wait_ge(S["qbd_ready"], a + 1)
                    at_least(pe, S["ln2_sum"], q)
                    for b in range(UB):
                        last = mm(W2[:, b * P:(b + 1) * P], ctT[:, b, :], wqkvo[:, 3, :],
                                  start=True, stop=True)
                    last.then_inc(S["proj"], 1)
                if route:
                    pe.wait_ge(S["onehot"], r + 1)
                    kw = dict(skip_group_check=True)
                    pos = CT[:, 0:UB * NE]
                    mm(pos, before[:, :], oh[:, :, :], start=True, stop=False, **kw)
                    mm(pos, ones_b[:, :], seen[:, mp, :].unsqueeze(1).to_broadcast([P, UB, NE]),
                       start=False, stop=False, **kw)
                    for t in range(1, UB):
                        last = mm(pos[:, t * NE:], ones_b[:, :], oh[:, 0:UB - t, :],
                                  start=False, stop=(t == UB - 1), **kw)
                    last.then_inc(S["pos_ready"], 1)
                if att:
                    score(UB * a + 2, 2)
                if mix:
                    pe.wait_ge(S["x1T_copied"], m + 1)
                    if post:
                        pe.wait_ge(S["ln2_sum"], q + 1)
                    elif att:
                        pe.wait_ge(S["qbd_ready"], a + 1)
                    if which[0] == -1:
                        pe.wait_ge(S["router_mm"], 1)
                    mm(W2, wqkvo[:, 0, :], x1T[:, :], start=True, stop=True).then_inc(S["q_ready"], 1)
                if att:
                    pe.wait_ge(ct_in_s[par], (k + 1) * 16)
                    for b in range(UB):
                        last = mm(W1[:, b * P:(b + 1) * P], ct_in[:, par, b * P:(b + 1) * P],
                                  wqkvo[:, 2, :], start=True, stop=True)
                    last.then_inc(S["v_ready"], 1)
                if gate:
                    pe.wait_ge(S["g_ready"], z + 1)
                    for b in range(UB):
                        for c in range(2):
                            last = mm(mixer_out[:, b * P:(b + 1) * P], g[:, c, b * P:(b + 1) * P], wout[:, c, :],
                                      start=(c == 0), stop=(c == 1))
                    last.then_inc(S["mixed"], 1)
                if att:
                    score(UB * a + 3, 3)
                if mix:
                    if att:
                        pe.wait_ge(S["v_copied"], a + 1)
                    km = k if par == 0 else k + 1
                    pe.wait_ge(ct_in_s[mp], (km + 1) * 16)
                    mm(W1, wqkvo[:, 1, :], ct_in[:, mp, :], start=True, stop=True).then_inc(S["k_ready"], 1)
                if att:
                    if route:
                        pe.wait_ge(S["idx_ready"], r + 1)
                    context(2)
                if att:
                    context(3)
                if mix:
                    score(UB * a + UB, UB)
                if post:
                    pe.wait_ge(S["x2_ready"], q + 1)
                    if gate:
                        pe.wait_ge(S["ln1_var"], z + 1)
                    for t in range(UB):
                        last = tr(W0[:, t * P:(t + 1) * P], x2[:, mp, t, 0:P], ident)
                    last.then_inc(S["x2T_ready"], 1)
                if post:
                    pe.wait_ge(S["x2T_copied"], q + 1)
                    if mix:
                        pe.wait_ge(S["qbd_ready"], m + 1)
                    elif att:
                        pe.wait_ge(S["qbd_ready"], a + 1)
                    for t in range(UB):
                        last = mm(W2[:, t * NE:(t + 1) * NE], x2T[:, t, :], wr[:, :], start=True, stop=True)
                    last.then_inc(S["logits"], 1)

            schedule(pe, unit)

            pe.wait_ge(S["idx_ready"], UN)
            mm(W0[:, 0:NE], ones_b[:, :], seen[:, 1, :], start=True, stop=True).then_inc(S["counts"], 1)

            XT, Y = ps[:, 0, 0:P], ps[:, 7, 0:P]
            pe.wait_ge(S["table_ready"], 1)
            pe.wait_ge(S["experts_in"], 32)
            pe.wait_ge(S["bias_back"], 32)

            def turn_rows(t, k, slot):
                pe.wait_ge(rows_in[slot], 16 * (k + 1))
                at_least(pe, S["rowT_copied"], t)
                tr(XT, xr[:, slot, 0:P], ident).then_inc(S["rowT"], 1)

            experts = {}
            turn_rows(0, 0, 0)

            def group(n, k, par):
                whole = isinstance(n, int)
                if whole and n == NG - 2 or not whole and par == 1:
                    experts.clear()
                for s in range(GT):
                    t = n * GT + s
                    if not whole or t < NT:
                        e = pe.value_load(tab[0:1, 1, bass.ds(t, 1)], min_val=0, max_val=NE - 1)
                        experts[s] = e
                        if not whole or t >= GT:
                            at_least(pe, S["gelu"], t - GT + 1)
                        mm(ps[:, 1 + s, :], ones3[:, :], bias[:, bass.ds(e * FF, FF)], start=True, stop=False)
                        pe.wait_ge(S["rowT_copied"], t + 1)
                        mm(ps[:, 1 + s, :], xrT[:, s, :], w1s[:, bass.ds(e * FF, FF)],
                           start=False, stop=True).then_inc(S["hidden"], 1)
                    if not whole or t + 1 < NT:
                        if s < 2:
                            turn_rows(t + 1, k, par * GT + s + 1)
                        else:
                            turn_rows(t + 1, k if par == 0 else k + 1, (1 - par) * GT)
                    if not whole or (1 <= t < NT + 1):
                        sb_ = (s - 1) % GT
                        pe.wait_ge(S["gelu"], t)
                        if not whole or t - 1 >= GT:
                            at_least(pe, S["hidT_copied"], t - GT)
                        for c in range(FC):
                            last = tr(ps[:, 4 + sb_, c * P:(c + 1) * P], hg[:, sb_, c * P:(c + 1) * P], ident)
                        last.then_inc(S["hidT"], 1)
                    if not whole or (2 <= t < NT + 2):
                        sc = (s - 2) % GT
                        if sc not in experts:
                            experts[sc] = pe.value_load(tab[0:1, 1, bass.ds(t - 2, 1)], min_val=0, max_val=NE - 1)
                        e = experts[sc]
                        if not whole or t > 2:
                            at_least(pe, S["res_ready"], t - 2)
                        mm(Y, ones3[:, :], bias[:, bass.ds(e * P + NE * FF, P)], start=True, stop=False)
                        pe.wait_ge(S["hidT_copied"], t - 1)
                        for c in range(FC):
                            last = mm(Y, hT[:, sc, c * P:(c + 1) * P], w2s[:, bass.ds(e * FF + c * P, P)],
                                      start=False, stop=(c == FC - 1))
                        last.then_inc(S["y_ready"], 1)

            schedule2(pe, group)

        @block.scalar
        def _(act):
            A = nc.scalar.activation
            link = Chain(act, S["act"])
            act.wait_ge(S["consts_in"], 80)
            link(A(dn[:, 0, :], alog[:, :, :].rearrange("p c n -> p (c n)"), ACT.Exp))
            act.wait_ge(S["delta_pre"], 1)
            A(v[:, 3, :], v[:, 2, :], ACT.Exp).then_inc(S["exp_a"], 1)
            act.wait_ge(S["exp_b"], 1)
            A(v[:, 5, :], v[:, 4, :], ACT.Ln).then_inc(S["ln_c"], 1)
            act.wait_ge(S["dax"], 1)
            A(dn[:, 3, :], dn[:, 2, :], ACT.Exp).then_inc(S["exp_a"], 1)

            def unit(a, k, par, which):
                z, m, q, r = a + 2, a + 1, a - 1, a - 2
                gate, mix, att, post, route = (runs(which, x) for x in (2, 1, 0, -1, -2))
                mp = 1 - par

                def exps(j):
                    i = UB * a + j
                    act.wait_ge(S["shifted"], i + 1)
                    A(E[:, j, :, :], E[:, j, :, :], ACT.Exp).then_inc(S["exp_ready"], 1)

                def heads(h0, h1):
                    for h in range(h0, h1):
                        last = A(qbd[:, mp, h, :, :], W2, ACT.Identity, scale=hmask[:, h:h + 1])
                    return last

                def gate_parts():
                    act.wait_ge(S["z_ready"], z + 1)
                    at_least(act, S["g_ready"], z)
                    if which[0] < 0:
                        A(sg[:, :, :], ps[:, 4:6, :], ACT.Tanh, scale=0.5).then_inc(S["gate_ready"], 1)
                        return
                    A(zs[:, :, :], ps[:, 4:6, :], ACT.Identity)
                    A(sg[:, :, :], ps[:, 4:6, :], ACT.Tanh, scale=0.5).then_inc(S["z_copied"], 1)
                    act.wait_ge(S["z_copied"], z + 1)
                    A(sg[:, :, :], sg[:, :, :], ACT.Identity, bias=ones_c).then_inc(S["gate_ready"], 1)

                if gate and which[0] < 0:
                    gate_parts()
                if mix:
                    act.wait_ge(S["ln1_shift"], m + 1)
                    at_least(act, S["x1T_ready"], m)
                    at_least(act, S["x1_kept"], m)
                    for b in range(UB):
                        last = A(x1[:, b, :], xs[:, b, :], ACT.Identity, bias=nb[:, b:b + 1], scale=rs[:, b:b + 1])
                    last.then_inc(S["x1_ready"], 1)
                if gate and which[0] >= 0:
                    gate_parts()
                if att:
                    exps(0)
                if post:
                    act.wait_ge(S["ctx_ready"], UB * a)
                    at_least(act, S["proj"], q)
                    A(ctT[:, :, :], CT, ACT.Identity).then_inc(S["ctx_copied"], 1)
                if mix:
                    act.wait_ge(S["x1T_ready"], m + 1)
                    at_least(act, S["q_ready"], m)
                    A(x1T[:, :], W1, ACT.Identity).then_inc(S["x1T_copied"], 1)
                if route:
                    act.wait_ge(S["diff_ready"], r + 1)
                    A(er[:, :, :], df[:, :, :], ACT.Exp).then_inc(S["gate_exp"], 1)
                if att:
                    exps(1)
                if att:
                    act.wait_ge(S["v_ready"], a + 1)
                    at_least(act, S["ctx_ready"], UB * (a - 1))
                    A(vbd[:, par, :, :].rearrange("p b (h w) -> p b h w", w=P + DH)[:, :, :, 0:DH],
                      W1, ACT.Identity).then_inc(S["v_copied"], 1)
                if mix:
                    act.wait_ge(S["q_ready"], m + 1)
                    at_least(act, S["scores"], UB * (m - 1) if not isinstance(m, int) or m > 1 else 0)
                    heads(0, H).then_inc(S["qbd_ready"], 1)
                    act.wait_ge(S["k_ready"], m + 1)
                    at_least(act, S["scores"], UB * m)
                    A(kt[:, :, :], W1, ACT.Identity).then_inc(S["k_copied"], 1)
                if att:
                    exps(2)
                if post:
                    act.wait_ge(S["ln2_shift"], q + 1)
                    if not isinstance(q, int) or q >= 2:
                        for t in range(UB):
                            act.wait_ge(rows_out[mp * UB + t], 16 * k)
                    for b in range(UB):
                        last = A(x2[:, mp, b, 0:P], xs2[:, b, :], ACT.Identity, bias=nb2[:, b:b + 1],
                                 scale=rs2[:, b:b + 1])
                    last.then_inc(S["x2_ready"], 1)
                if post:
                    act.wait_ge(S["x2T_ready"], q + 1)
                    at_least(act, S["logits"], q)
                    A(x2T[:, :, :], W0, ACT.Identity).then_inc(S["x2T_copied"], 1)
                if att:
                    exps(3)

            schedule(act, unit)

            act.wait_ge(S["counts"], 2)
            for e in range(NE // 2, NE):
                at = act.value_load(pad_at[0:1, e:e + 1], min_val=0, max_val=NE * CAP)
                act.dma_start(lists[bass.ds(at, P), :], pad[:, :]).then_inc(S["pads_out"], 16)

            def copy_rows(t, s):
                act.wait_ge(S["rowT"], t + 1)
                if not isinstance(t, int) or t >= GT:
                    at_least(act, S["hidden"], t - GT + 1)
                A(xrT[:, s, :], ps[:, 0, 0:P], ACT.Identity).then_inc(S["rowT_copied"], 1)

            copy_rows(0, 0)

            def group(n, k, par):
                whole = isinstance(n, int)
                for s in range(GT):
                    t = n * GT + s
                    if not whole or t < NT:
                        act.wait_ge(S["hidden"], t + 1)
                        if not whole or t >= GT:
                            at_least(act, S["hidT"], t - GT + 1)
                        A(hg[:, s, :], ps[:, 1 + s, :], ACT.Gelu).then_inc(S["gelu"], 1)
                    if not whole or t + 1 < NT:
                        copy_rows(t + 1, (s + 1) % GT)
                    if s < 2 and (not whole or 2 <= n):
                        act.wait_ge(S["shift3"], n - 1)
                        for slot in range(par * GT + s, par * GT + 2 * s + 1):
                            if not whole or n >= 4:
                                act.wait_ge(final_out[slot], 16 * (k - 1))
                            A(ot[:, slot, :], rsd[:, slot, :], ACT.Identity, bias=nb3[:, slot:slot + 1],
                              scale=rs3[:, slot:slot + 1]).then_inc(S["out_ready"], 1)

            schedule2(act, group)

        @block.vector
        def _(dve):
            V = nc.vector
            link = Chain(dve, S["dve"])
            V.memset(ones_f[:, :], 1.0).then_inc(S["ones_done"], 1)
            V.memset(ones_b[:, :], 1.0)
            V.memset(mh[:, :], -0.5)
            V.memset(g8[:, 19:20], 0.5)
            link(V.memset(seen[:, :, :], 0.0))
            V.memset(dn[:, 7, :], 0.0)
            V.memset(pad[:, 0:P + 1], 0.0)
            link(V.memset(pad[:, P + 1:ROW], float(2 * TOK)))
            V.tensor_copy(pad[:, P:P + 1], pad[:, 0:1]).then_inc(S["pad_ready"], 1)
            dve.wait_ge(S["consts_in"], 80)
            V.tensor_copy(x2[:, 0, :, P + 1], ids)
            V.tensor_scalar(x2[:, 1, :, P + 1], ids, float(UT), None, ALU.add)
            link(V.tensor_copy(before[:, :], before_f))
            dve.wait_ge(S["mix_rows"], 1)
            V.tensor_copy(dbc[:, :], W0[:, 0:96])
            V.tensor_copy(dlt[:, :], W1[0:RANK, 0:1]).then_inc(S["mix_rows_copied"], 1)
            dve.wait_ge(S["delta_raw"], 1)
            link(V.tensor_tensor(v[:, 0, :], W2[:, 0:2], sm[:, 0:2], ALU.add))
            link(V.tensor_scalar(v[:, 1, :], v[:, 0, :], -1.0, None, ALU.mult))
            V.tensor_tensor(v[:, 2, :], v[:, 0, :], v[:, 1, :], ALU.min).then_inc(S["delta_pre"], 1)
            dve.wait_ge(S["exp_a"], 1)
            V.tensor_scalar(v[:, 4, :], v[:, 3, :], 1.0, None, ALU.add).then_inc(S["exp_b"], 1)
            dve.wait_ge(S["weights_in"], 80)
            link(V.tensor_tensor(g8[:, 0:16], wgs[:, :], wgs[:, :], ALU.mult))
            V.tensor_reduce(g8[:, 16:17], g8[:, 0:16], AX.X, ALU.add).then_inc(S["router_norm"], 1)
            dve.wait_ge(S["ln_c"], 1)
            dve.wait_ge(S["exp_b"], 1)
            link(V.tensor_scalar(v[:, 6, :], v[:, 4, :], -1.0, None, ALU.add))
            V.tensor_scalar(v[:, 7, :], v[:, 6, :], 0.0, None, ALU.is_le)
            link(V.tensor_scalar(v[:, 8, :], v[:, 6, :], 1e-30, None, ALU.max))
            link(V.reciprocal(v[:, 9, :], v[:, 8, :]))
            link(V.tensor_tensor(v[:, 10, :], v[:, 9, :], v[:, 5, :], ALU.mult))
            link(V.tensor_tensor(v[:, 11, :], v[:, 10, :], v[:, 7, :], ALU.add))
            link(V.tensor_tensor(v[:, 12, :], v[:, 11, :], v[:, 3, :], ALU.mult))
            link(V.scalar_tensor_tensor(v[:, 13, :], v[:, 0, :], 0.0, v[:, 12, :], ALU.max, ALU.add))
            delta = v[:, 13, :].unsqueeze(2).to_broadcast([P, 2, NST])
            dve.wait_ge(S["act"], 1)
            dn3 = dn[:, :, :].rearrange("p k (c n) -> p k c n", c=2)
            link(V.tensor_tensor(dn3[:, 1], dn3[:, 0], delta, ALU.mult))
            V.tensor_scalar(dn[:, 2, :], dn[:, 1, :], -1.0, None, ALU.mult).then_inc(S["dax"], 1)
            link(V.tensor_tensor(dn[:, 4, 0:NST], dbc[:, RANK:RANK + NST], dbc[:, RANK + NST:96], ALU.mult))
            pw3 = pw[:, :, :].rearrange("p (c n) t -> p c n t", c=2)
            link(V.tensor_tensor(pw3[:, :, :, 0], dn[:, 4, 0:NST].unsqueeze(1).to_broadcast([P, 2, NST]), delta, ALU.mult))
            dve.wait_ge(S["exp_a"], 2)
            w, src = 1, 3
            while w < P:
                link(V.tensor_tensor(pw[:, :, w:2 * w], pw[:, :, 0:w],
                                     dn[:, src, :].unsqueeze(2).to_broadcast([P, 2 * NST, w]), ALU.mult))
                nxt = {3: 5, 5: 6, 6: 5}[src]
                if 2 * w < P:
                    link(V.tensor_tensor(dn[:, nxt, :], dn[:, src, :], dn[:, src, :], ALU.mult))
                w, src = 2 * w, nxt
            link(V.tensor_reduce(wsum[:, :, :], pw3.rearrange("p c n t -> p c t n"), AX.X, ALU.add))
            for c in range(2):
                last = V.tensor_tensor_scan(yd[:, c, :], wsum[:, c, :], pw[:, 0, :], 0.0, ALU.add, ALU.bypass)
            link(last)
            for c in range(2):
                last = V.tensor_scalar(yd[:, c, :], yd[:, c, :], sm[:, 2 + c:3 + c], 0.5, ALU.add, ALU.mult)
            last.then_inc(S["yd_ready"], 1)

            def router():
                dve.wait_ge(S["router_pow"], 1)
                link(V.tensor_scalar(g8[:, 18:19], g8[:, 17:18], 1e-4, None, ALU.max))
                link(V.reciprocal(g8[:, 18:19], g8[:, 18:19]))
                V.tensor_scalar(g8[:, 0:16], wgs[:, :], g8[:, 18:19], None, ALU.mult).then_inc(S["router_norm"], 1)
                dve.wait_ge(S["wg_turned"], 1)
                V.tensor_copy(wgT[:, :], CT[0:16, 0:NE]).then_inc(S["wgT_ready"], 1)
                dve.wait_ge(S["router_mm"], 1)
                link(V.tensor_copy(wr[:, :], CT[:, 16:16 + NE]))
                dve.wait_ge(S["bias_in"], 16)
                for n in range(3):
                    link(V.tensor_copy(bp[:, n, :], bf[:, n, :]))
                    if n < 2:
                        link(V.tensor_tensor(bf[:, n + 1, :], bf[:, n, :], bp[:, n, :], ALU.subtract))
                V.tensor_copy(pr[:, 0, :], wr[:, :]).then_inc(S["bias_out"], 1)

            def variance(st, mv, ve, done):
                V.tensor_tensor(mv[:, 0], st[:, :, 1], st[:, :, 4], ALU.add)
                V.tensor_tensor(mv[:, 1], st[:, :, 1], st[:, :, 4], ALU.subtract)
                link(V.scalar_tensor_tensor(mv[:, 2], st[:, :, 2], P * EPS, st[:, :, 5], ALU.add, ALU.add))
                link(V.scalar_tensor_tensor(mv[:, 3], mv[:, 1], 0.25, mv[:, 1], ALU.mult, ALU.mult))
                V.scalar_tensor_tensor(ve, mv[:, 2], 1.0 / P, mv[:, 3], ALU.mult, ALU.add).then_inc(done, 1)

            def layer_norm(xs, st, mv, ve, done):
                for b in range(UB):
                    last = V.bn_stats(st[:, b, :], xs[:, b, :])
                link(last)
                variance(st, mv, ve[:, :], done)

            def unit(a, k, par, which):
                z, m, q, r = a + 2, a + 1, a - 1, a - 2
                gate, mix, att, post, route = (runs(which, x) for x in (2, 1, 0, -1, -2))
                mp = 1 - par
                mixer_out = ps[:, 4 + which[0], :] if which[0] < 0 else W0
                lg = W2[:, 0:UB * NE].rearrange("p (t e) -> p t e", t=UB)
                pos = CT[:, 0:UB * NE].rearrange("p (t e) -> p t e", t=UB)

                def maximum(j):
                    i = UB * a + j
                    dve.wait_ge(S["scores"], i + 1)
                    pp = 2 * (j % 2)
                    link(V.tensor_reduce(mx[:, :], ps[:, pp:pp + 2, :].rearrange("p g (h q) -> p q (g h)", h=4),
                                         AX.X, ALU.max))

                def shift(j):
                    i = UB * a + j
                    pp = 2 * (j % 2)
                    at_least(dve, S["ctx_ready"], i - 3)
                    V.tensor_tensor(E[:, j, :, :], ps[:, pp:pp + 2, :].rearrange("p g (h q) -> p (g h) q", h=4),
                                    mx[:, :].unsqueeze(1).to_broadcast([P, H, P]),
                                    ALU.subtract).then_inc(S["shifted"], 1)

                def inverse(j):
                    i = UB * a + j
                    jj, pp = (j - 1) % UB, (j - 1) % 2
                    dve.wait_ge(S["exp_ready"], i)
                    at_least(dve, S["attn_ready"], i - 2)
                    link(V.tensor_reduce(se[:, pp, :], E[:, jj, :, :].rearrange("p h q -> p q h"), AX.X, ALU.add))
                    V.reciprocal(re[:, pp, :], se[:, pp, :]).then_inc(S["recip_ready"], 1)

                if route:
                    dve.wait_ge(S["logits"], r + 1)
                    link(V.tensor_reduce(r4[:, 0, :], lg, AX.X, ALU.max))
                    V.tensor_tensor(df[:, :, :], lg, r4[:, 0, :].unsqueeze(2).to_broadcast([P, UB, NE]),
                                    ALU.subtract).then_inc(S["diff_ready"], 1)
                    dve.wait_ge(S["diff_ready"], r + 1)
                    link(V.scalar_tensor_tensor(rk[:, :, :].rearrange("p t e -> p (t e)"),
                                                df[:, :, :].rearrange("p t e -> p (t e)"), 0.0, rank,
                                                ALU.is_ge, ALU.mult))
                    link(V.tensor_reduce(r4[:, 1, :], rk[:, :, :], AX.X, ALU.max))
                    link(V.tensor_tensor(oh[:, :, :], rank.rearrange("p (t e) -> p t e", t=UB),
                                         r4[:, 1, :].unsqueeze(2).to_broadcast([P, UB, NE]), ALU.is_equal))
                    V.tensor_reduce(cu[:, :], oh[:, :, :].rearrange("p t e -> p e t"), AX.X,
                                    ALU.add).then_inc(S["onehot"], 1)
                if post:
                    inverse(0)
                if which[0] == UN:
                    jj = UB - 1
                    dve.wait_ge(S["recip_ready"], UB * UN)
                    dve.wait_ge(S["ctx_ready"], UB * UN - 1)
                    V.tensor_tensor(E[:, jj, :, :], E[:, jj, :, :],
                                    re[:, jj % 2, :].unsqueeze(1).to_broadcast([P, H, P]),
                                    ALU.mult).then_inc(S["attn_ready"], 1)
                if att:
                    maximum(0)
                    shift(0)
                if which[0] < 0 and gate:
                    dve.wait_ge(S["gate_ready"], z + 1)
                    V.scalar_tensor_tensor(zs[:, :, :], sg[:, :, :], 1.0, ps[:, 4:6, :], ALU.add,
                                           ALU.mult).then_inc(S["z_copied"], 1)
                if which[0] == -2:
                    router()
                if att:
                    inverse(1)
                    maximum(1)
                    shift(1)
                if post:
                    dve.wait_ge(S["proj"], q + 1)
                    at_least(dve, S["x2_ready"], q)
                    dve.wait_ge(S["x1_kept"], q + 1)
                    V.tensor_tensor(xs2[:, :, :], W2.rearrange("p (b d) -> p b d", b=UB),
                                    x1r[:, mp, :, :], ALU.add).then_inc(S["ln2_sum"], 1)
                    dve.wait_ge(S["ln2_sum"], q + 1)
                    layer_norm(xs2, st2, mv2, ve2, S["ln2_var"])
                if route:
                    at_least(dve, S["onehot"], r + 1)
                    V.tensor_tensor(seen[:, par, :], seen[:, mp, :], cu[:, :], ALU.add)
                    dve.wait_ge(S["pos_ready"], r + 1)
                    link(V.tensor_tensor(pr[:, :, :], pos, oh[:, :, :], ALU.mult))
                    link(V.tensor_reduce(r4[:, 2, :], pr[:, :, :], AX.X, ALU.add))
                    link(V.scalar_tensor_tensor(r4[:, 3, :], r4[:, 1, :], float(-CAP), r4[:, 2, :],
                                                ALU.mult, ALU.add))
                    dve.wait_ge(S["gate_exp"], r + 1)
                    link(V.tensor_reduce(r4[:, 4, :], er[:, :, :], AX.X, ALU.add))
                    V.reciprocal(x2[:, par, :, P], r4[:, 4, :])
                    link(V.tensor_scalar(x2[:, par, :, P + 1], x2[:, par, :, P + 1], float(2 * UT), None, ALU.add))
                    V.tensor_scalar(idx[:, par, :], r4[:, 3, :], float(NE * CAP), None,
                                    ALU.add).then_inc(S["idx_ready"], 1)
                if att:
                    inverse(2)
                if post:
                    dve.wait_ge(S["ln2_rstd"], q + 1)
                    V.scalar_tensor_tensor(nb2[:, :], mv2[:, 0], -0.5, rs2[:, :], ALU.mult,
                                           ALU.mult).then_inc(S["ln2_shift"], 1)
                if att:
                    maximum(2)
                    shift(2)
                if gate:
                    dve.wait_ge(S["mixed"], z + 1)
                    dve.wait_ge(xk_in[par], 16 * (k + 2))
                    at_least(dve, S["x1_ready"], z)
                    link(V.tensor_tensor(xs[:, :, :], mixer_out.rearrange("p (b d) -> p b d", b=UB),
                                         xk[:, par, :].rearrange("p (b d) -> p b d", b=UB), ALU.add))
                    layer_norm(xs, st, mv, ve, S["ln1_var"])
                if att:
                    inverse(3)
                    maximum(3)
                if gate:
                    dve.wait_ge(S["ln1_rstd"], z + 1)
                    V.scalar_tensor_tensor(nb[:, :], mv[:, 0], -0.5, rs[:, :], ALU.mult,
                                           ALU.mult).then_inc(S["ln1_shift"], 1)
                if att:
                    shift(3)
                if mix:
                    dve.wait_ge(S["x1_ready"], m + 1)
                    V.tensor_copy(x1r[:, mp, :, :], x1[:, :, :]).then_inc(S["x1_kept"], 1)

            schedule(dve, unit, link, VECTOR_STEPS)

            dve.wait_ge(S["counts"], 1)
            link(V.tensor_copy(cn[:, 0, :], W0[:, 0:NE]))
            link(V.tensor_scalar(cn[0:1, 1, :], rank[0:1, 0:NE], float(-CAP), float(NE * CAP), ALU.mult, ALU.add))
            V.tensor_tensor(pad_at[:, :], cn[0:1, 1, :], cn[0:1, 0, :], ALU.add).then_inc(S["counts"], 1)
            link(V.tensor_scalar(cn[0:1, 3, :], cn[0:1, 0, :], float(P - 1), 1.0 / P, ALU.add, ALU.mult))
            link(V.tensor_scalar(cni[:, :], cn[0:1, 3, :], 1.0 / 256 - 0.5, None, ALU.add))
            link(V.tensor_copy(cn[0:1, 4, :], cni[:, :]))
            link(V.tensor_tensor_scan(cn[0:1, 5, :], cn[0:1, 4, :], cn[0:1, 4, :], 0.0, ALU.add, ALU.bypass))
            g3 = ge[:, :, :].rearrange("p k (t e) -> p k t e", e=NE)
            link(V.tensor_tensor(g3[:, 0], tnum.rearrange("p (t e) -> p t e", e=NE),
                                 cn[0:1, 5, :].unsqueeze(1).to_broadcast([1, NT, NE]), ALU.is_ge))
            link(V.tensor_reduce(tb[:, 0, :], g3[:, 0], AX.X, ALU.add))
            link(V.tensor_tensor(g3[:, 1], g3[:, 0],
                                 cn[0:1, 4, :].unsqueeze(1).to_broadcast([1, NT, NE]), ALU.mult))
            link(V.tensor_reduce(tb[:, 1, :], g3[:, 1], AX.X, ALU.add))
            link(V.tensor_tensor(tb[:, 2, :], tnum.rearrange("p (t e) -> p t e", e=NE)[:, :, 0], tb[:, 1, :], ALU.subtract))
            link(V.tensor_scalar(tb[:, 3, :], tb[:, 0, :], float(CAP), None, ALU.mult))
            link(V.scalar_tensor_tensor(tb[:, 4, :], tb[:, 2, :], float(P), tb[:, 3, :], ALU.mult, ALU.add))
            link(V.tensor_scalar(tab[:, 0, :], tb[:, 4, :], float(NE * CAP), None, ALU.min))
            V.tensor_scalar(tab[:, 1, :], tb[:, 0, :], float(NE - 1), None, ALU.min).then_inc(S["table_ready"], 1)

            def group(n, k, par):
                whole = isinstance(n, int)
                for s in range(GT):
                    t = n * GT + s
                    if s == 0 and (not whole or n >= 2):
                        dve.wait_ge(S["rstd3"], n - 1)
                        lo, hi = par * GT, par * GT + GT
                        V.scalar_tensor_tensor(nb3[:, lo:hi], mv3[:, 0, lo:hi], -0.5, rs3[:, lo:hi],
                                               ALU.mult, ALU.mult).then_inc(S["shift3"], 1)
                    if not whole or 1 <= t < NT + 1:
                        sb_ = (s - 1) % GT
                        dve.wait_ge(S["hidT"], t)
                        if not whole or t - 1 >= GT:
                            at_least(dve, S["y_ready"], t - GT)
                        V.tensor_copy(hT[:, sb_, :], ps[:, 4 + sb_, :]).then_inc(S["hidT_copied"], 1)
                    if not whole or 2 <= t < NT + 2:
                        slot = (par * GT + s - 2) % NX
                        dve.wait_ge(S["y_ready"], t - 1)
                        if not whole or t - 2 >= NX:
                            at_least(dve, S["out_ready"], t - 2 - NX + 1)
                        V.tensor_copy(tnew[:, slot:slot + 1], xr[:, slot, P + 1:ROW])
                        V.scalar_tensor_tensor(rsd[:, slot, :], ps[:, 7, 0:P], xr[:, slot, P:P + 1],
                                               xr[:, slot, 0:P], ALU.mult, ALU.add).then_inc(S["res_ready"], 1)
                        dve.wait_ge(S["res_ready"], t - 1)
                        link(V.bn_stats(st3[:, slot, :], rsd[:, slot, :]))
                    if s == 1 and (not whole or 1 <= n <= NG):
                        lo = (1 - par) * GT
                        variance(st3[:, lo:lo + GT, :], mv3[:, :, lo:lo + GT], ve3[:, lo:lo + GT], S["var3"])
                        if not whole or n >= 3:
                            for slot in range(lo, lo + GT):
                                dve.wait_ge(final_out[slot], 16 * (k if par == 1 else k - 1))
                        link(V.tensor_copy(tix[:, lo:lo + GT], tnew[:, lo:lo + GT]))

            schedule2(dve, group, link, VECTOR_STEPS_2)

        @block.gpsimd
        def _(pool):
            G = nc.gpsimd
            G.memset(ones3[:, :], 0.0).then_inc(S["memset_done"], 1)
            pool.wait_ge(S["memset_done"], 1)
            G.memset(ones3[0:3, :], 1.0).then_inc(S["memset_done"], 1)
            G.iota(tailx[:, :], pattern=[[QR, UB]], base=NE * CAP, channel_multiplier=1).then_inc(S["memset_done"], 1)
            G.memset(bias[:, :], 0.0).then_inc(S["memset_done"], 1)
            G.memset(vbd[:, 0, :, :], 0.0)
            pool.wait_ge(S["router_norm"], 1)
            G.tensor_tensor(g8[:, 17:18], g8[:, 16:17], g8[:, 19:20], ALU.pow).then_inc(S["router_pow"], 1)
            G.memset(vbd[:, 1, :, :], 0.0).then_inc(S["memset_done"], 1)
            pool.wait_ge(S["pad_ready"], 1)
            pool.wait_ge(S["memset_done"], 5)
            for t in range(UB):
                G.indirect_dma_start(out=lists, out_offset=bass.IndirectOffsetOnAxis(ap=tailx[:, t:t + 1], axis=0),
                                     in_=pad[0:QR, :], in_offset=None).then_inc(rows_out[UB + t], 16)

            def unit(a, k, par, which):
                z, m, q, r = a + 2, a + 1, a - 1, a - 2
                gate, mix, att, post, route = (runs(which, x) for x in (2, 1, 0, -1, -2))
                mp = 1 - par

                def normalize(j):
                    i = UB * a + j
                    jj, pp = (j - 1) % UB, (j - 1) % 2
                    pool.wait_ge(S["recip_ready"], i)
                    G.tensor_tensor(E[:, jj, :, :], E[:, jj, :, :],
                                    re[:, pp, :].unsqueeze(1).to_broadcast([P, H, P]),
                                    ALU.mult).then_inc(S["attn_ready"], 1)

                def scatter(first, count):
                    if route:
                        for t in range(first, first + count):
                            G.indirect_dma_start(
                                out=lists, out_offset=bass.IndirectOffsetOnAxis(ap=idx[:, par, t:t + 1], axis=0),
                                in_=x2[:, par, t, :], in_offset=None).then_inc(rows_out[par * UB + t], 16)

                if post and which[0] < UN:
                    normalize(0)
                if gate:
                    pool.wait_ge(S["z_copied"], z + 1)
                    if which[0] == -2:
                        pool.wait_ge(S["yd_ready"], 1)
                    scaled = g if which[0] < 0 else zs
                    if which[0] < 0:
                        at_least(pool, S["mixed"], z)
                    for c in range(2):
                        last = G.tensor_tensor(scaled[:, c, :].rearrange("p (b l) -> p b l", b=UB),
                                               zs[:, c, :].rearrange("p (b l) -> p b l", b=UB),
                                               yd[:, c, :].unsqueeze(1).to_broadcast([P, UB, P]), ALU.mult)
                    if which[0] < 0:
                        last.then_inc(S["g_ready"], 1)
                    else:
                        last.then_inc(S["z_scaled"], 1)
                        pool.wait_ge(S["z_scaled"], z - 1)
                        pool.wait_ge(S["gate_ready"], z + 1)
                        at_least(pool, S["mixed"], z)
                        G.tensor_tensor(g[:, :, :], zs[:, :, :], sg[:, :, :], ALU.mult).then_inc(S["g_ready"], 1)
                if att:
                    normalize(1)
                if post:
                    pool.wait_ge(S["ln2_var"], q + 1)
                    at_least(pool, S["x2_ready"], q)
                    if route and att:
                        pool.wait_ge(S["idx_ready"], r + 1)
                    G.tensor_tensor(rs2[:, :], ve2[:, :], mh[:, :], ALU.pow).then_inc(S["ln2_rstd"], 1)
                if att:
                    normalize(2)
                if route and not att:
                    pool.wait_ge(S["idx_ready"], r + 1)
                scatter(0, 2)
                if gate:
                    pool.wait_ge(S["ln1_var"], z + 1)
                    at_least(pool, S["x1_ready"], z)
                    G.tensor_tensor(rs[:, :], ve[:, :], mh[:, :], ALU.pow).then_inc(S["ln1_rstd"], 1)
                if att:
                    normalize(3)
                scatter(2, 2)

            schedule(pool, unit)

            def group(n, k, par):
                whole = isinstance(n, int)
                def power():
                    if not whole or 1 <= n <= NG:
                        lo = (1 - par) * GT
                        pool.wait_ge(S["var3"], n)
                        if not whole:
                            pool.wait_ge(S["out_ready"], (n - 1) * GT)
                        G.tensor_tensor(rs3[:, lo:lo + GT], ve3[:, lo:lo + GT], mh[:, 0:GT],
                                        ALU.pow).then_inc(S["rstd3"], 1)

                if not whole or n < NG:
                    power()
                if not whole or 2 <= n:
                    if whole:
                        pool.wait_ge(S["out_ready"], (n - 1) * GT)
                    for s in range(GT):
                        slot = par * GT + s
                        G.indirect_dma_start(
                            out=out, out_offset=bass.IndirectOffsetOnAxis(ap=tix[:, slot:slot + 1], axis=0),
                            in_=ot[:, slot, :], in_offset=None, bounds_check=TOK - 1,
                            oob_is_err=False).then_inc(final_out[slot], 16)
                if whole and n >= NG:
                    power()

            schedule2(pool, group)
            for slot in range(NX):
                pool.wait_ge(final_out[slot], 16 * ((NG + (slot < GT)) // 2))
            for n, q in enumerate(rows_out):
                pool.wait_ge(q, 16 * (UN // 2 + n // UB))
            pool.wait_ge(S["pads_out"], 16 * NE)
            pool.wait_ge(S["bias_back"], 32)


VECTOR_STEPS = 48
VECTOR_STEPS_2 = 12


def constants():
    f = np.float32
    p = np.arange(P)
    hmask = (p[:, None] // DH == np.arange(H)[None, :]).astype(f) * f(DH ** -0.5)
    rank = np.tile(NE - np.arange(NE), UB)[None, :].repeat(P, 0).astype(f)
    ids = (p[:, None] + P * np.arange(UB)[None, :] - 2 * UT).astype(f)
    tnum = np.repeat(np.arange(NT), NE)[None, :].repeat(P, 0).astype(f)
    before = (p[:, None] < p[None, :]).astype(f)
    rest = np.zeros((P, 4), f)
    rest[:, 0], rest[:, 1] = 1.0, -0.5
    return np.ascontiguousarray(np.concatenate(
        [np.eye(P, dtype=f), before, hmask, rank, ids, tnum, rest], 1))


def kernel(x, ctx_1024, L0_attn_W_in, L0_attn_conv_w, L0_attn_conv_b, L0_attn_W_x, L0_attn_W_dt,
           L0_attn_b_dt, L0_attn_A_log, L0_attn_D_skip, L0_attn_W_out, L0_xattn_W_Q, L0_xattn_W_K,
           L0_xattn_W_V, L0_xattn_W_O, L0_ffn_w_red, L0_ffn_wg, L0_ffn_w1, L0_ffn_b1, L0_ffn_w2, L0_ffn_b2):
    import concourse.bacc as bacc
    from concourse.bass_utils import run_bass_kernel_spmd

    def c(a):
        return np.ascontiguousarray(a)

    x, ctx_1024 = np.asarray(x), np.asarray(ctx_1024)
    chunks = lambda a: c(np.asarray(a).reshape(2, P, -1).transpose(1, 0, 2))
    t = lambda a: np.asarray(a).T
    w1, w2 = np.asarray(L0_ffn_w1), np.asarray(L0_ffn_w2)
    ins = {
        "x_t": c(x.transpose(2, 0, 1).reshape(P, TOK)),
        "x_tok": c(x.transpose(1, 0, 2).reshape(P, TOK)),
        "ctx_t": c(ctx_1024.transpose(2, 0, 1).reshape(P, TOK)),
        "wz_t": c(t(L0_attn_W_in)[:, EI:]),
        "wx_t": chunks(t(L0_attn_W_x)),
        "wdt_t": c(t(L0_attn_W_dt)),
        "small": c(np.concatenate([np.asarray(L0_attn_b_dt).reshape(2, P).T,
                                   np.asarray(L0_attn_D_skip).reshape(2, P).T], 1)),
        "a_log": chunks(L0_attn_A_log),
        "wout_t": chunks(t(L0_attn_W_out)),
        "wqkvo_t": c(np.stack([t(L0_xattn_W_Q), t(L0_xattn_W_K), t(L0_xattn_W_V), t(L0_xattn_W_O)], 1)),
        "wred_t": c(t(L0_ffn_w_red)),
        "wg": c(np.asarray(L0_ffn_wg)),
        "w1": c(w1.transpose(1, 0, 2).reshape(P, NE * FF)),
        "w2": c(w2.reshape(NE, FC, P, P).transpose(2, 0, 1, 3).reshape(P, NE * FC * P)),
        "b12": c(np.concatenate([np.asarray(L0_ffn_b1).reshape(-1), np.asarray(L0_ffn_b2).reshape(-1)]).reshape(P, -1)),
        "consts": constants(),
    }
    nc = bacc.Bacc("TRN2", target_bir_lowering=False, num_devices=1)
    args = [nc.dram_tensor("in_" + n, a.shape, mybir.dt.from_np(a.dtype), kind="ExternalInput").ap()
            for n, a in ins.items()]
    out = nc.dram_tensor("out", [TOK, P], F32, kind="ExternalOutput").ap()
    decoder_program(nc, *args, out)
    r = run_bass_kernel_spmd(nc, [{"in_" + n: a for n, a in ins.items()}], core_ids=[0])
    return r.results[0]["out"].reshape(NSEQ, P, P)
```
